# Optimizing a Trainium2 kernel written in Bass

```python
import numpy as np
import jax
import jax.numpy as jnp

def _softmax(x, axis=-1):
    return jax.nn.softmax(x, axis=axis)

def _gelu(x):
    return jax.nn.gelu(x, approximate=True)

def _silu(x):
    return jax.nn.silu(x)

def _sigmoid(x):
    return jax.nn.sigmoid(x)

def _layernorm(x, axis=-1, eps=1e-05):
    m = jnp.mean(x, axis=axis, keepdims=True)
    v = jnp.var(x, axis=axis, keepdims=True)
    return (x - m) / jnp.sqrt(v + eps)

def _scatter_add(tgt, idx, src, axis=0):
    return tgt.at[idx].add(src)

def _segment_sum(src, seg, n):
    return jax.ops.segment_sum(src, seg, n)
kernel_name = 'mk_seq_postln_d1_jaxref_r8_cfa84f'

def setup_inputs(seed: int=0):
    np.random.seed(seed)
    _w = jnp.asarray

    def _L0_attn_setup():
        import jax, jax.numpy as jnp
        import numpy as np
        D_MODEL = 128
        NUM_HEADS = 16
        HEAD_DIM = D_MODEL // NUM_HEADS
        THETA = 10000.0
        B, T = (4, 256)

        def _cos_sin(seq_len, head_dim, theta):
            freqs = 1.0 / theta ** (jnp.arange(0, head_dim, 2, dtype=jnp.float32) / head_dim)
            t = jnp.arange(seq_len, dtype=jnp.float32)
            angles = jnp.outer(t, freqs)
            return jnp.concatenate([jnp.cos(angles), jnp.sin(angles)], axis=-1)

        def _apply_rope(x, cos_sin):
            x1 = x[..., 0::2]
            x2 = x[..., 1::2]
            half = x.shape[-1] // 2
            cos = cos_sin[:, :half]
            sin = cos_sin[:, half:]
            out = jnp.stack([x1 * cos - x2 * sin, x1 * sin + x2 * cos], axis=-1)
            return out.reshape(x.shape)
        key = jax.random.key(seed)
        k1, k2, k3 = jax.random.split(key, 3)
        x = jax.random.normal(k1, (B, T, D_MODEL), dtype=jnp.float32)
        W_qkv = jax.random.normal(k2, (3 * D_MODEL, D_MODEL), dtype=jnp.float32) * D_MODEL ** (-0.5)
        W_out = jax.random.normal(k3, (D_MODEL, D_MODEL), dtype=jnp.float32) * D_MODEL ** (-0.5)
        return {'x': x, 'W_qkv': W_qkv, 'W_out': W_out}
    _L0_attn_in = _L0_attn_setup()

    def _L0_ffn_setup():
        import jax, jax.numpy as jnp
        import numpy as np
        DIM = 128

        def _reference_tuple_inner(x, W_r, W_k, W_v, mu_r, mu_k):
            B, T, C = x.shape
            x_prev = jnp.concatenate([jnp.zeros((B, 1, C), x.dtype), x[:, :-1, :]], axis=1)
            xr = mu_r * x + (1.0 - mu_r) * x_prev
            xk = mu_k * x + (1.0 - mu_k) * x_prev
            r = jax.nn.sigmoid(jnp.einsum('btc,dc->btd', xr, W_r))
            k = jnp.einsum('btc,dc->btd', xk, W_k)
            k_act = jnp.square(jax.nn.relu(k))
            out = r * jnp.einsum('btc,dc->btd', k_act, W_v)
            new_state = x[:, -1, :]
            return (out, new_state)
        key = jax.random.key(seed)
        ks = jax.random.split(key, 6)
        B, T, C = (8, 256, DIM)
        x = jax.random.normal(ks[0], (B, T, C), dtype=jnp.float32)
        s = 1.0 / np.sqrt(C)
        W_r = jax.random.uniform(ks[1], (C, C), jnp.float32, -s, s)
        W_k = jax.random.uniform(ks[2], (C, C), jnp.float32, -s, s)
        W_v = jax.random.uniform(ks[3], (C, C), jnp.float32, -s, s)
        mu_r = jax.random.uniform(ks[4], (C,), jnp.float32)
        mu_k = jax.random.uniform(ks[5], (C,), jnp.float32)
        return {'x': x, 'W_r': W_r, 'W_k': W_k, 'W_v': W_v, 'mu_r': mu_r, 'mu_k': mu_k}
    _L0_ffn_in = _L0_ffn_setup()
    _d = {'L0_attn_x': _L0_attn_in['x'], 'L0_attn_W_qkv': _L0_attn_in['W_qkv'], 'L0_attn_W_out': _L0_attn_in['W_out'], 'L0_ffn_W_r': _L0_ffn_in['W_r'], 'L0_ffn_W_k': _L0_ffn_in['W_k'], 'L0_ffn_W_v': _L0_ffn_in['W_v'], 'L0_ffn_mu_r': _L0_ffn_in['mu_r'], 'L0_ffn_mu_k': _L0_ffn_in['mu_k']}
    _x0 = _d['L0_attn_x']
    _d['L0_attn_x'] = jax.random.normal(jax.random.fold_in(jax.random.key(seed), 1), (8, 512, 128), dtype=_x0.dtype)
    del _x0
    return _d

def reference(L0_attn_x, L0_attn_W_qkv, L0_attn_W_out, L0_ffn_W_r, L0_ffn_W_k, L0_ffn_W_v, L0_ffn_mu_r, L0_ffn_mu_k):

    def _L0_attn_ref(x, W_qkv, W_out):
        import jax, jax.numpy as jnp
        import numpy as np
        D_MODEL = 128
        NUM_HEADS = 16
        HEAD_DIM = D_MODEL // NUM_HEADS
        THETA = 10000.0
        B, T = (4, 256)

        def _cos_sin(seq_len, head_dim, theta):
            freqs = 1.0 / theta ** (jnp.arange(0, head_dim, 2, dtype=jnp.float32) / head_dim)
            t = jnp.arange(seq_len, dtype=jnp.float32)
            angles = jnp.outer(t, freqs)
            return jnp.concatenate([jnp.cos(angles), jnp.sin(angles)], axis=-1)

        def _apply_rope(x, cos_sin):
            x1 = x[..., 0::2]
            x2 = x[..., 1::2]
            half = x.shape[-1] // 2
            cos = cos_sin[:, :half]
            sin = cos_sin[:, half:]
            out = jnp.stack([x1 * cos - x2 * sin, x1 * sin + x2 * cos], axis=-1)
            return out.reshape(x.shape)
        Bsz, Tlen, _ = x.shape
        qkv = jnp.einsum('bti,oi->bto', x, W_qkv)
        qkv = qkv.reshape(Bsz, Tlen, 3 * NUM_HEADS, HEAD_DIM).transpose(0, 2, 1, 3)
        q, k, v = jnp.split(qkv, 3, axis=1)
        cos_sin = _cos_sin(Tlen, HEAD_DIM, THETA)
        q = _apply_rope(q, cos_sin)
        k = _apply_rope(k, cos_sin)
        scores = jnp.einsum('bhqd,bhkd->bhqk', q, k) / np.sqrt(HEAD_DIM).astype(np.float32)
        causal = jnp.tril(jnp.ones((Tlen, Tlen), dtype=bool))
        scores = jnp.where(causal[None, None], scores, -jnp.inf)
        attn = jax.nn.softmax(scores, axis=-1)
        o = jnp.einsum('bhqk,bhkd->bhqd', attn, v)
        o = o.transpose(0, 2, 1, 3).reshape(Bsz, Tlen, D_MODEL)
        return jnp.einsum('bti,oi->bto', o, W_out)

    def _L0_ffn_ref(x, W_r, W_k, W_v, mu_r, mu_k):
        import jax, jax.numpy as jnp
        import numpy as np
        DIM = 128

        def _reference_tuple_inner(x, W_r, W_k, W_v, mu_r, mu_k):
            B, T, C = x.shape
            x_prev = jnp.concatenate([jnp.zeros((B, 1, C), x.dtype), x[:, :-1, :]], axis=1)
            xr = mu_r * x + (1.0 - mu_r) * x_prev
            xk = mu_k * x + (1.0 - mu_k) * x_prev
            r = jax.nn.sigmoid(jnp.einsum('btc,dc->btd', xr, W_r))
            k = jnp.einsum('btc,dc->btd', xk, W_k)
            k_act = jnp.square(jax.nn.relu(k))
            out = r * jnp.einsum('btc,dc->btd', k_act, W_v)
            new_state = x[:, -1, :]
            return (out, new_state)
        return _reference_tuple_inner(x, W_r, W_k, W_v, mu_r, mu_k)[0]
    x = L0_attn_x
    x = _layernorm(x + _L0_attn_ref(x, L0_attn_W_qkv, L0_attn_W_out), axis=-1)
    x = _layernorm(x + _L0_ffn_ref(x, L0_ffn_W_r, L0_ffn_W_k, L0_ffn_W_v, L0_ffn_mu_r, L0_ffn_mu_k), axis=-1)
    return x

_drawn_inputs = setup_inputs


def setup_inputs(seed=0):
    import zlib

    import numpy as np

    out = dict(_drawn_inputs(seed))
    spreads = {}
    factors = {'L0_ffn_W_r': 3.17, 'L0_ffn_mu_r': 6.286}
    for name, (base, spread) in spreads.items():
        noise = np.random.default_rng([zlib.crc32(name.encode()), seed]).standard_normal(out[name].shape)
        drawn = base * np.exp(spread * noise) if base else spread * noise
        out[name] = jnp.asarray(drawn.astype(out[name].dtype))
    for name, factor in factors.items():
        out[name] = (out[name] * factor).astype(out[name].dtype)
    return out
```

```python
import concourse.bass as bass
from concourse import mybir
from contextlib import ExitStack

B, T, D = 8, 512, 128
H, HD = 16, 8
G = 4
NG = H // G
NB = T // 128
NN = B * NG
PARTS = 3
KR = PARTS * PARTS * HD
KM = KR + PARTS
VW = 32
EPS = 1e-5
NEG = -3.0e38
SCALE = float(HD) ** -0.5


def attention_block(nc, x, w_qkv, w_out, w_r, w_k, w_v, mu_r, mu_k, rope_cos, rope_sin, eye, causal,
                    q_parts, k_parts, out):
    f32 = mybir.dt.float32
    bf16 = mybir.dt.bfloat16
    ALU = mybir.AluOpType
    ACT = mybir.ActivationFunctionType
    AX = mybir.AxisListType

    x_rows = x.rearrange("b (i p) d -> b p i d", p=128)
    out_rows = out.rearrange("b (i p) d -> b p i d", p=128)

    ctx = ExitStack()
    with ctx:
        def sb(name, shape, dt=f32):
            return ctx.enter_context(nc.sbuf_tensor(name, shape, dt))

        def sem(name):
            return ctx.enter_context(nc.semaphore(name))

        ident = sb("ident", [128, 128])
        ident_b = sb("ident_b", [128, 128], bf16)
        mask = sb("mask", [128, 128])
        mask_b = sb("mask_b", [128, 128], bf16)
        cos = sb("cos", [128, T])
        sin = sb("sin", [128, T])
        w_rows = sb("w_rows", [128, 7, 128])
        wq_t = sb("wq_t", [128, 2, 128])
        wk_t = sb("wk_t", [128, 2, 128])
        wv_t = sb("wv_t", [128, 128])
        wo_t = sb("wo_t", [128, 128])
        ffn_t = sb("ffn_t", [128, 3, 128])
        mu = sb("mu", [128, 2])
        mu_rest = sb("mu_rest", [128, 2])
        z_all = sb("z_all", [128, B * NB, 128])
        v_all = sb("v_all", [128, B * NB, 128])
        stats = sb("stats", [128, B * NB, 6])
        mean = sb("mean", [128, B * NB])
        rstd = sb("rstd", [128, B * NB])
        half = sb("half", [128, B * NB])
        var = sb("var", [128, B * NB])
        std = sb("std", [128, B * NB])
        x_in = sb("x_in", [128, 2, NB, 128])
        xt = sb("xt", [128, 2, T])
        rot_a = sb("rot_a", [128, 2, T])
        rot_b = sb("rot_b", [128, 2, T])
        rot = sb("rot", [128, 2, T])
        rest = sb("rest", [128, 2, T])
        split = sb("split", [128, 2, 2, PARTS, T], bf16)
        qa = sb("qa", [KM, NG, G * T], bf16)
        ka = sb("ka", [KM, NG, G * T], bf16)
        vs = sb("vs", [128, NG, NB, G, VW])
        probs = sb("probs", [128, 2, 10, 512])
        nmax = sb("nmax", [128, 2, G * NB])
        nmax_rest = sb("nmax_rest", [128, G * NB])
        nsplit = sb("nsplit", [128, 2, 128], bf16)
        nmax_t = sb("nmax_t", [PARTS * G * NB, 2, 128], bf16)
        o_raw = sb("o_raw", [128, T])
        den_inv = sb("den_inv", [128, NB, G])
        o_tok = sb("o_tok", [128, NB, H, HD])
        o_t = sb("o_t", [128, T])
        x1 = sb("x1", [128, 2, NB, 128])
        x1_t = sb("x1_t", [128, 2, T + 1])
        scaled = sb("scaled", [128, 2, T])
        mixed = sb("mixed", [128, 2, 2, T])
        k_relu = sb("k_relu", [128, T])
        k_sq = sb("k_sq", [128, 2, T])
        gate_e = sb("gate_e", [128, T])
        gate_d = sb("gate_d", [128, T])
        gate = sb("gate", [128, T])
        gated = sb("gated", [128, T])

        bank = [ctx.enter_context(nc.psum_tensor(f"bank{i}", [128, 512], f32)) for i in range(2)]
        wide = [ctx.enter_context(nc.psum_tensor(f"wide{i}", [128, 1024], f32)) for i in range(2)]
        ps_o = ctx.enter_context(nc.psum_tensor("ps_o", [128, 512], f32))
        ps_m = ctx.enter_context(nc.psum_tensor("ps_m", [128, 512], f32))
        ps_x = ps_m
        ps_qk = [wide[0][:, 0:512], wide[0][:, 512:1024], wide[1][:, 0:512], wide[1][:, 512:1024]]
        ps_v = ps_o

        S = {n: sem(n) for n in (
            "weights_in consts_in z_in mu_in fills ident_cast w_ps w_ready mu_ready "
            "xt_ps xt_ready proj_done q_mul qs_mul k_mul ks_mul q_ps qs_ps k_ps ks_ps "
            "v_ps v_ready "
            "p1_ready p1_reduced ns_chain ns_ready mt_ps mt_ready "
            "p2_ready exp_done v_slot mask_done av_done o_ready ot_raw_ps den_ready o_normed "
            "otok_ps ot_ready y_ps z_ready z_stats "
            "norm_chain var_ready std_ready norm_ready x1_ready x1_ps x1t_ready scaled_r scaled_k "
            "mix_r mix_k kps rps relu_done sq_done exp_gate gate_one gate_inv vps2 gated_done z2_ready "
            "z2_stats out_ready stored").split()}
        x_in_ld = [sem(f"x_in_ld{s}") for s in range(2)]
        rot_done = [sem(f"rot_done_{u}") for u in "qk"]
        hi_done = [sem(f"hi_done_{u}") for u in "qk"]
        rest_done = [sem(f"rest_done_{u}") for u in "qk"]
        mid_done = [sem(f"mid_done_{u}") for u in "qk"]
        lo_done = [sem(f"lo_done_{u}") for u in "qk"]
        parked = [[sem(f"parked_{u}{s}") for s in range(2)] for u in "qk"]
        qk_ld = [sem(f"qk_ld{c}") for c in range(NG)]
        max_ld = [sem(f"max_ld{c}") for c in range(NG)]

        block = ctx.enter_context(nc.Block())

        mul_of = [S["q_mul"], S["qs_mul"], S["k_mul"], S["ks_mul"]]
        ps_of = [S["q_ps"], S["qs_ps"], S["k_ps"], S["ks_ps"]]

        def pairs(eng, turn):
            for s in range(2):
                turn(s, 0, s, True)
            with eng.Fori(1, B // 2 - 1) as i:
                for s in range(2):
                    turn(2 * i + s, i, s, True)
            for s in range(2):
                turn(B - 2 + s, B // 2 - 1, s, s == 0)

        def groups(eng, step):
            for b in (-1, 0):
                for c in range(NG):
                    step(b, c)
            with eng.Fori(1, B - 1) as b:
                for c in range(NG):
                    step(b, c)
            for c in range(NG):
                step(B - 1, c)

        def ahead(b, c, lead):
            bb, cc = b + (c + lead) // NG, (c + lead) % NG
            n = NG * bb + cc
            if isinstance(n, int) and not 0 <= n < NN:
                return None
            return n, bb, cc

        P1 = [(3, 0, 2, 1), (3, 2, 2, 1), (2, 0, 2, 1), (2, 2, 2, 1), (1, 0, 4, 2), (0, 0, 4, 4)]

        @block.sync
        def _(sp):
            sp.dma_start(w_rows[:, 0:3, :], w_qkv.rearrange("(a p) c -> p a c", p=128)).then_inc(S["weights_in"], 16)
            sp.dma_start(ident[:, :], eye).then_inc(S["consts_in"], 16)
            for s in range(2):
                sp.dma_start(x_in[:, s], x_rows[s]).then_inc(x_in_ld[s], 16)
            for a, w in ((3, w_out), (4, w_r), (5, w_k), (6, w_v)):
                sp.dma_start(w_rows[:, a, :], w).then_inc(S["weights_in"], 16)
            sp.dma_start(mask[:, :], causal).then_inc(S["consts_in"], 16)
            sp.dma_start(cos[:, :], rope_cos).then_inc(S["consts_in"], 16)
            sp.dma_start(sin[:, :], rope_sin).then_inc(S["consts_in"], 16)
            sp.dma_start(mu[:, 0:1], mu_r.rearrange("(p a) -> p a", a=1)).then_inc(S["mu_in"], 16)
            sp.dma_start(mu[:, 1:2], mu_k.rearrange("(p a) -> p a", a=1)).then_inc(S["mu_in"], 16)
            sp.dma_start(z_all[:, :, :], x.rearrange("b (i p) d -> p (b i) d", p=128)).then_inc(S["z_in"], 16)

            def park(n, i, s, more):
                if more and not (isinstance(n, int) and n >= B - 2):
                    sp.wait_ge(S["xt_ps"], n + 1)
                    sp.dma_start(x_in[:, s], x_rows[n + 2]).then_inc(x_in_ld[s], 16)
                for u, parts in enumerate((q_parts, k_parts)):
                    sp.wait_ge(lo_done[u], n + 1)
                    for c in range(NG):
                        sp.dma_start(parts[n, c].rearrange("a p t -> p a t"),
                                     split[32 * c:32 * c + 32, u, s]).then_inc(parked[u][s], 16)

            pairs(sp, park)
            for u in range(2):
                for s in range(2):
                    sp.wait_ge(parked[u][s], 16 * NG * (B // 2))

            sp.wait_ge(S["fills"], 4)

            def feed(b, c):
                g = ahead(b, c, 4)
                if g:
                    n, bb, cc = g
                    if not isinstance(b, int) or b >= 0:
                        sp.wait_ge(S["p2_ready"], 10 * (n - 3))
                    def rows(parts, lo, hi):
                        return parts[bb, cc, lo:hi].rearrange("a (d g) t -> (a d) (g t)", g=G)
                    for r in range(PARTS):
                        at = 24 * r
                        sp.dma_start(ka[at:at + 24, cc, :], rows(k_parts, 0, 3)).then_inc(qk_ld[cc], 16)
                        n1 = 3 - r
                        sp.dma_start(qa[at:at + 8 * n1, cc, :], rows(q_parts, r, 3)).then_inc(qk_ld[cc], 16)
                        if r:
                            sp.dma_start(qa[at + 8 * n1:at + 24, cc, :], rows(q_parts, 0, r)).then_inc(qk_ld[cc], 16)
                g = ahead(b, c, 2)
                if g:
                    n, bb, cc = g
                    sp.wait_ge(S["mt_ready"], n + 1)
                    for p in range(PARTS):
                        sp.dma_start(qa[KR + p:KR + p + 1, cc, :].rearrange("o (x q) -> o x q", q=128),
                                     nmax_t[16 * p:16 * p + 16, cc % 2, :]).then_inc(max_ld[cc], 16)

            groups(sp, feed)

            with sp.Fori(0, B) as b:
                sp.wait_ge(S["out_ready"], b + 1)
                sp.dma_start(out_rows[b], z_all[:, bass.ds(b * NB, NB), :]).then_inc(S["stored"], 16)
            sp.wait_ge(S["stored"], 16 * B)

        @block.tensor
        def _(pe):
            pe.wait_ge(S["weights_in"], 16 * 5)
            pe.wait_ge(S["consts_in"], 16 * 4)
            for a in range(7):
                mm = pe.transpose((bank[0] if a < 4 else bank[1])[:, 128 * (a % 4):128 * (a % 4) + 128],
                                  w_rows[:, a, :], ident[:, :])
            mm.then_inc(S["w_ps"], 1)

            def x_transposes(n, i, s):
                pe.wait_ge(x_in_ld[s], 16 * (i + 1))
                pe.wait_ge(S["xt_ready"], n)
                for j in range(NB):
                    mm = pe.transpose(ps_x[:, 128 * j:128 * j + 128], x_in[:, s, j, :], ident[:, :])
                mm.then_inc(S["xt_ps"], 1)

            def project(n, i, s, more):
                pe.wait_ge(S["xt_ready"], n + 1)
                for a, w in enumerate((wq_t[:, 0, :], wq_t[:, 1, :], wk_t[:, 0, :], wk_t[:, 1, :])):
                    pe.wait_ge(mul_of[a], n)
                    pe.matmul(ps_qk[a], w, xt[:, s, :], start=True, stop=True).then_inc(ps_of[a], 1)
                    if a == 1 and more:
                        x_transposes(n + 1, i + s, 1 - s)
                pe.wait_ge(S["v_ready"], n)
                for j in range(NB):
                    mm = pe.matmul(ps_v[:, 128 * j:128 * j + 128], xt[:, s, 128 * j:128 * j + 128],
                                   wv_t[:, :], start=True, stop=True)
                mm.then_inc(S["v_ps"], 1)

            x_transposes(0, 0, 0)
            pe.wait_ge(S["w_ready"], 9)
            pairs(pe, project)

            for m in mul_of:
                pe.wait_ge(m, B)
            pe.wait_ge(S["v_ready"], B)
            pe.wait_ge(S["ident_cast"], 2)

            def p1_tile(g, t):
                n, bb, cc = g
                if t == 0:
                    pe.wait_ge(qk_ld[cc], 16 * 8 * (bb + 1))
                if not (isinstance(n, int) and n == 0 and t < 2):
                    pe.wait_ge(S["p1_reduced"], 6 * n + t - 1)
                i, g0, heads, per = P1[t]
                keys = 128 * (i + 1)
                for h in range(heads):
                    at = 512 * (h // per) + keys * (h % per)
                    tok = T * (g0 + h)
                    pe.matmul(wide[t % 2][:, at:at + keys], qa[0:KR, cc, tok + 128 * i:tok + keys],
                              ka[0:KR, cc, tok:tok + keys], start=True, stop=False)
                    mm = pe.matmul(wide[t % 2][:, at + keys - 128:at + keys], ident_b[:, :], mask_b[:, :],
                                   start=False, stop=True)
                mm.then_inc(S["p1_ready"], 1)

            def p2_tile(g, t):
                n, bb, cc = g
                if t == 0:
                    pe.wait_ge(max_ld[cc], 16 * PARTS * (bb + 1))
                if not (isinstance(n, int) and n == 0 and t < 2):
                    pe.wait_ge(S["exp_done"], 10 * n + t - 1)

                def block_of(h, j, at):
                    tok = T * h
                    return pe.matmul(bank[t % 2][:, at:at + T - 128 * j],
                                     ka[0:KM, cc, tok + 128 * j:tok + 128 * j + 128],
                                     qa[0:KM, cc, tok + 128 * j:tok + T], start=True, stop=True)
                if t < 4:
                    mm = block_of(t, 0, 0)
                elif t < 8:
                    block_of(t - 4, 1, 0)
                    mm = block_of(t - 4, 3, 384)
                else:
                    block_of(2 * (t - 8), 2, 0)
                    mm = block_of(2 * (t - 8) + 1, 2, 256)
                mm.then_inc(S["p2_ready"], 1)

            def p_block(par, h, j):
                if j == 0:
                    return probs[:, par, h, :]
                if j == 1:
                    return probs[:, par, 4 + h, 0:384]
                if j == 3:
                    return probs[:, par, 4 + h, 384:512]
                return probs[:, par, 8 + h // 2, 256 * (h % 2):256 * (h % 2) + 256]

            def av(g, j):
                n, bb, cc = g
                if j == 0:
                    pe.wait_ge(S["mask_done"], 3 * (n + 1))
                    pe.wait_ge(S["v_slot"], n + 1)
                    pe.wait_ge(S["o_ready"], n)
                for h in range(G):
                    mm = pe.matmul(ps_o[32 * h:32 * h + 32, 128 * j:T], vs[:, cc, j, h, :],
                                   p_block(cc % 2, h, j), start=(j == 0), stop=(j == NB - 1))
                if j == NB - 1:
                    mm.then_inc(S["av_done"], 1)

            def small_bank_free(b, c):
                g = ahead(b, c, 0)
                if g:
                    pe.wait_ge(S["o_normed"], g[0])
                    if c == 0:
                        pe.wait_ge(S["z_ready"], g[1])

            def max_transpose(g):
                n, bb, cc = g
                pe.wait_ge(S["ns_ready"], n + 1)
                pe.transpose(ps_m[:, 0:64].bitcast(bf16), nsplit[:, cc % 2, :], ident_b[:, :]).then_inc(S["mt_ps"], 1)

            def o_transposes(g):
                n, bb, cc = g
                pe.wait_ge(S["o_ready"], n + 1)
                for j in range(NB):
                    mm = pe.transpose(ps_m[:, 128 * j:128 * j + 128], o_raw[:, 128 * j:128 * j + 128], ident[:, :])
                mm.then_inc(S["ot_raw_ps"], 1)

            def step(b, c):
                new, scored, mult, maxed, post = (ahead(b, c, k) for k in (4, 2, 1, 3, 0))

                def p1(t):
                    if new:
                        p1_tile(new, t)

                def p2(t):
                    if scored:
                        p2_tile(scored, t)

                def pv(j):
                    if mult:
                        av(mult, j)

                p2(0)
                p1(0)
                small_bank_free(b, c)
                if maxed:
                    max_transpose(maxed)
                p2(1)
                pv(0)
                p1(1)
                p2(2)
                if maxed:
                    pe.wait_ge(S["mt_ready"], maxed[0] + 1)
                if post:
                    o_transposes(post)
                p2(3)
                pv(1)
                p1(2)
                p2(4)
                p1(3)
                p2(5)
                pv(2)
                if post and c == NG - 1:
                    pe.wait_ge(S["o_normed"], post[0] + 1)
                    for j in range(NB):
                        mm = pe.transpose(ps_m[:, 128 * j:128 * j + 128],
                                          o_tok[:, j].rearrange("p h d -> p (h d)"), ident[:, :])
                    mm.then_inc(S["otok_ps"], 1)
                p1(4)
                p2(6)
                p2(7)
                pv(3)
                p1(5)
                p2(8)
                if post and c == NG - 1:
                    pe.wait_ge(S["ot_ready"], post[1] + 1)
                    for j in range(NB):
                        mm = pe.matmul(ps_m[:, 128 * j:128 * j + 128], o_t[:, 128 * j:128 * j + 128],
                                       wo_t[:, :], start=True, stop=True)
                    mm.then_inc(S["y_ps"], 1)
                p2(9)

            groups(pe, step)

            pe.wait_ge(S["z_ready"], B)

            def channel_mix(n, i, s, more):
                xk = wide[s][:, 0:512]
                rv = wide[s][:, 512:1024]
                pe.wait_ge(S["x1_ready"], n + 1)
                pe.wait_ge(S["relu_done"], n)
                for j in range(NB):
                    mm = pe.transpose(xk[:, 128 * j:128 * j + 128], x1[:, s, j, :], ident[:, :])
                mm.then_inc(S["x1_ps"], 1)
                pe.wait_ge(S["mix_r"], n + 1)
                pe.wait_ge(S["gated_done"], n)
                for j in range(NB):
                    mm = pe.matmul(rv[:, 128 * j:128 * j + 128], mixed[:, s, 0, 128 * j:128 * j + 128],
                                   ffn_t[:, 0, :], start=True, stop=True)
                mm.then_inc(S["rps"], 1)
                pe.wait_ge(S["mix_k"], n + 1)
                pe.matmul(xk, ffn_t[:, 1, :], mixed[:, s, 1, :], start=True, stop=True).then_inc(S["kps"], 1)
                pe.wait_ge(S["sq_done"], n + 1)
                pe.wait_ge(S["exp_gate"], n + 1)
                for j in range(NB):
                    mm = pe.matmul(rv[:, 128 * j:128 * j + 128], k_sq[:, s, 128 * j:128 * j + 128],
                                   ffn_t[:, 2, :], start=True, stop=True)
                mm.then_inc(S["vps2"], 1)

            pairs(pe, channel_mix)

        @block.scalar
        def _(act):
            def copy(dst, src):
                return act.activation(dst, src, ACT.Copy)

            act.wait_ge(S["w_ps"], 1)
            for a, w in ((0, wq_t), (1, wk_t)):
                src = bank[0][:, 128 * a:128 * a + 128].rearrange("p (c g d) -> p c g d", g=G, d=HD)
                for c in range(NG):
                    plain = w[:, 0, 32 * c:32 * c + 32].rearrange("p (d g) -> p g d", g=G)
                    first = copy(plain, src[:, c])
                    if c == NG - 1:
                        first.then_inc(S["w_ready"], 1)
                    swap = w[:, 1, 32 * c:32 * c + 32].rearrange("p (e f g) -> p g e f", f=2, g=G)
                    pair = src[:, c].rearrange("p g (e f) -> p g e f", f=2)
                    for f in range(2):
                        last = copy(swap[:, :, :, f], pair[:, :, :, 1 - f])
                        if c == NG - 1:
                            last.then_inc(S["w_ready"], 1)
            copy(wv_t[:, :], bank[0][:, 256:384]).then_inc(S["w_ready"], 1)
            copy(wo_t[:, :], bank[0][:, 384:512]).then_inc(S["w_ready"], 1)
            copy(ffn_t[:, :, :], bank[1][:, 0:384].rearrange("p (a n) -> p a n", a=3)).then_inc(S["w_ready"], 1)

            def evacuate_xt(n, i, s):
                act.wait_ge(S["xt_ps"], n + 1)
                if not (isinstance(n, int) and n < 2):
                    act.wait_ge(S["v_ps"], n - 1)
                copy(xt[:, s, :], ps_x[:, :]).then_inc(S["xt_ready"], 1)

            def split_parts(n, i, s, more):
                for u in range(2):
                    act.wait_ge(rot_done[u], n + 1)
                    act.wait_ge(parked[u][s], 16 * NG * i)
                    copy(split[:, u, s, 0], rot[:, u, :]).then_inc(hi_done[u], 1)
                    if u == 0 and more:
                        evacuate_xt_next(n, i, s)
                for u in range(2):
                    act.wait_ge(rest_done[u], n + 1)
                    copy(split[:, u, s, 1], rest[:, u, :]).then_inc(mid_done[u], 1)
                act.wait_ge(S["v_ps"], n + 1)
                copy(v_all[:, bass.ds(n * NB, NB), :].rearrange("p i d -> p (i d)"), ps_v[:, :]).then_inc(S["v_ready"], 1)

            def evacuate_xt_next(n, i, s):
                act.wait_ge(S["xt_ps"], n + 2)
                if not (isinstance(n, int) and n < 1):
                    act.wait_ge(S["v_ps"], n)
                copy(xt[:, 1 - s, :], ps_x[:, :]).then_inc(S["xt_ready"], 1)

            evacuate_xt(0, 0, 0)
            pairs(act, split_parts)

            def step(b, c):
                scored, mult, post = (ahead(b, c, k) for k in (2, 1, 0))

                def exps(t0, t1):
                    if not scored:
                        return
                    n, bb, cc = scored
                    for t in range(t0, t1):
                        if t == 0 and not (isinstance(n, int) and n < 2):
                            act.wait_ge(S["av_done"], n - 1)
                        act.wait_ge(S["p2_ready"], 10 * n + t + 1)
                        act.activation(probs[:, cc % 2, t, :], bank[t % 2][:, :], ACT.Exp,
                                       scale=SCALE).then_inc(S["exp_done"], 1)

                exps(0, 7)
                if post and c == NG - 1:
                    act.wait_ge(S["otok_ps"], post[1] + 1)
                    act.wait_ge(S["y_ps"], post[1])
                    copy(o_t[:, :], ps_m[:, :]).then_inc(S["ot_ready"], 1)
                exps(7, 9)
                if mult:
                    n = mult[0]
                    act.wait_ge(S["av_done"], n + 1)
                    act.wait_ge(S["ot_raw_ps"], n)
                    copy(o_raw[:, :], ps_o[:, :]).then_inc(S["o_ready"], 1)
                exps(9, 10)

            groups(act, step)

            def root(k):
                act.wait_ge(S["var_ready"], k)
                act.activation(std[:, :], var[:, :], ACT.Sqrt).then_inc(S["std_ready"], 1)

            root(1)

            def mix(n, i, s, more):
                xk = wide[s][:, 0:512]
                rv = wide[s][:, 512:1024]
                act.wait_ge(S["x1_ps"], n + 1)
                if not (isinstance(n, int) and n < 2):
                    act.wait_ge(S["mix_k"], n - 1)
                copy(x1_t[:, s, 1:T + 1], xk).then_inc(S["x1t_ready"], 1)
                act.wait_ge(S["x1t_ready"], n + 1)
                act.wait_ge(S["mu_ready"], 1)
                act.wait_ge(S["mix_r"], n)
                act.activation(scaled[:, 0, :], x1_t[:, s, 1:T + 1], ACT.Copy, scale=mu[:, 0:1]).then_inc(S["scaled_r"], 1)
                act.wait_ge(S["rps"], n + 1)
                act.wait_ge(S["gate_one"], n)
                act.activation(gate_e[:, :], rv, ACT.Exp, scale=-1.0).then_inc(S["exp_gate"], 1)
                act.wait_ge(S["kps"], n + 1)
                act.wait_ge(S["sq_done"], n)
                act.activation(k_relu[:, :], xk, ACT.Relu).then_inc(S["relu_done"], 1)

            pairs(act, mix)
            root(2)

        @block.vector
        def _(dve):
            dve.memset(vs[:, :, :, :, :], 1.0).then_inc(S["fills"], 1)
            dve.memset(x1_t[:, :, 0:1], 0.0).then_inc(S["fills"], 1)
            dve.memset(nsplit[:, :, :], 0.0).then_inc(S["fills"], 1)
            dve.memset(ka[64:KM, :, :], 1.0).then_inc(S["fills"], 1)
            dve.wait_ge(S["consts_in"], 16 * 4)
            dve.wait_ge(S["mu_in"], 32)
            dve.tensor_copy(ident_b[:, :], ident[:, :]).then_inc(S["ident_cast"], 1)
            dve.tensor_copy(mask_b[:, :], mask[:, :]).then_inc(S["ident_cast"], 1)
            dve.tensor_scalar(mu_rest[:, :], mu[:, :], -1.0, 1.0, ALU.mult, ALU.add).then_inc(S["mu_ready"], 1)

            def rotate(n, i, s, more):
                for a in range(4):
                    u = a // 2
                    dve.wait_ge(ps_of[a], n + 1)
                    dve.wait_ge(rot_done[u], n)
                    dst, table = ((rot_a, cos), (rot_b, sin))[a % 2]
                    dve.tensor_tensor(dst[:, u, :], ps_qk[a], table[:, :], ALU.mult).then_inc(mul_of[a], 1)
                for u in range(2):
                    dve.wait_ge(hi_done[u], n + 1)
                    dve.wait_ge(lo_done[u], n)
                    dve.tensor_tensor(rest[:, u, :], rot[:, u, :], split[:, u, s, 0], ALU.subtract).then_inc(rest_done[u], 1)

            pairs(dve, rotate)

            def step(b, c):
                new, maxed, post = (ahead(b, c, k) for k in (4, 3, 0))

                def reduce(t):
                    if not new:
                        return
                    n, bb, cc = new
                    if t == 0 and not (isinstance(n, int) and n < 2):
                        dve.wait_ge(S["ns_ready"], n - 1)
                    dve.wait_ge(S["p1_ready"], 6 * n + t + 1)
                    i, g0, heads, per = P1[t]
                    keys = 128 * (i + 1)
                    src = wide[t % 2][:, 0:512 * (heads // per)].rearrange("p (k n) -> p k n", n=512)[:, :, 0:keys * per]
                    dst = nmax[:, cc % 2, :].rearrange("p (g i) -> p g i", i=NB)[:, g0:g0 + heads, i]
                    if per > 1:
                        src = wide[t % 2][:, 0:keys * heads].rearrange("p (h m) -> p h m", m=keys)
                    dve.tensor_reduce(dst, src, AX.X, ALU.max, negate=True).then_inc(S["p1_reduced"], 1)

                reduce(0)
                if maxed:
                    n, bb, cc = maxed
                    dve.wait_ge(S["mt_ps"], n + 1)
                    if not (isinstance(n, int) and n < 2):
                        b2, c2 = bb + (cc - 2) // NG, (cc - 2) % NG
                        dve.wait_ge(max_ld[c2], 16 * PARTS * (b2 + 1))
                    dve.tensor_copy(nmax_t[:, cc % 2, :], ps_m[0:PARTS * G * NB, 0:64].bitcast(bf16)).then_inc(S["mt_ready"], 1)
                reduce(1)
                if post:
                    n, bb, cc = post
                    o = ps_m[:, :].rearrange("p (j g w) -> p j g w", j=NB, g=G)
                    dve.wait_ge(S["ot_raw_ps"], n + 1)
                    dve.wait_ge(S["o_normed"], n)
                    dve.wait_ge(S["otok_ps"], bb)
                    dve.reciprocal(den_inv[:, :, :], o[:, :, :, HD]).then_inc(S["den_ready"], 1)
                    dve.wait_ge(S["den_ready"], n + 1)
                    dve.tensor_tensor(o_tok[:, :, G * cc:G * cc + G, :], o[:, :, :, 0:HD],
                                      den_inv[:, :, :].unsqueeze(3).to_broadcast((128, NB, G, HD)), ALU.mult).then_inc(S["o_normed"], 1)
                for t in range(2, 6):
                    reduce(t)
                if post and c == NG - 1:
                    bb = post[1]
                    if isinstance(bb, int) and bb == 0 or not isinstance(bb, int):
                        dve.wait_ge(S["z_in"], 16)
                    dve.wait_ge(S["y_ps"], bb + 1)
                    z = z_all[:, bass.ds(bb * NB, NB), :]
                    dve.tensor_tensor(z, ps_m[:, :].rearrange("p (i d) -> p i d", i=NB), z, ALU.add).then_inc(S["z_ready"], 1)
                    dve.wait_ge(S["z_ready"], bb + 1)
                    for j in range(NB):
                        dve.bn_stats(stats[:, bass.ds(bb * NB + j, 1), :].rearrange("p a k -> p (a k)"),
                                     z_all[:, bass.ds(bb * NB + j, 1), :].rearrange("p a d -> p (a d)")).then_inc(S["z_stats"], 1)

            groups(dve, step)

            chain = [0]

            def link(ins):
                chain[0] += 1
                ins.then_inc(S["norm_chain"], 1)
                dve.wait_ge(S["norm_chain"], chain[0])

            def norms(k):
                m_even, q_even, m_odd, q_odd = (stats[:, :, a] for a in (1, 2, 4, 5))
                link(dve.tensor_tensor(half[:, :], m_even, m_odd, ALU.subtract))
                link(dve.tensor_scalar(half[:, :], half[:, :], 0.5, None, ALU.mult))
                link(dve.tensor_tensor(mean[:, :], half[:, :], m_odd, ALU.add))
                link(dve.tensor_tensor(half[:, :], half[:, :], half[:, :], ALU.mult))
                link(dve.tensor_tensor(var[:, :], q_even, q_odd, ALU.add))
                link(dve.tensor_scalar(var[:, :], var[:, :], 1.0 / D, EPS, ALU.mult, ALU.add))
                dve.tensor_tensor(var[:, :], var[:, :], half[:, :], ALU.add).then_inc(S["var_ready"], 1)
                dve.wait_ge(S["std_ready"], k)
                dve.reciprocal(rstd[:, :], std[:, :]).then_inc(S["norm_ready"], 1)
                dve.wait_ge(S["norm_ready"], k)

            dve.wait_ge(S["z_stats"], B * NB)
            norms(1)

            def normalise(n, j, dst):
                at = n * NB + j
                return dve.tensor_scalar(dst, z_all[:, bass.ds(at, 1), :].rearrange("p a d -> p (a d)"),
                                         mean[:, bass.ds(at, 1)], rstd[:, bass.ds(at, 1)], ALU.subtract, ALU.mult)

            def mix(n, i, s, more):
                rv = wide[s][:, 512:1024]
                if not (isinstance(n, int) and n < 2):
                    dve.wait_ge(S["z2_ready"], n - 1)
                    dve.wait_ge(S["x1_ps"], n - 1)
                for j in range(NB):
                    last = normalise(n, j, x1[:, s, j, :])
                last.then_inc(S["x1_ready"], 1)
                if not (isinstance(n, int) and n < 2):
                    dve.wait_ge(S["kps"], n - 1)
                dve.wait_ge(S["scaled_r"], n + 1)
                dve.scalar_tensor_tensor(out=mixed[:, s, 0, :], in0=x1_t[:, s, 0:T], scalar=mu_rest[:, 0:1],
                                         in1=scaled[:, 0, :], op0=ALU.mult, op1=ALU.add).then_inc(S["mix_r"], 1)
                dve.wait_ge(S["scaled_k"], n + 1)
                dve.scalar_tensor_tensor(out=mixed[:, s, 1, :], in0=x1_t[:, s, 0:T], scalar=mu_rest[:, 1:2],
                                         in1=scaled[:, 1, :], op0=ALU.mult, op1=ALU.add).then_inc(S["mix_k"], 1)
                dve.wait_ge(S["exp_gate"], n + 1)
                dve.wait_ge(S["gate_inv"], n)
                dve.tensor_scalar(gate_d[:, :], gate_e[:, :], 1.0, None, ALU.add).then_inc(S["gate_one"], 1)
                dve.wait_ge(S["gate_one"], n + 1)
                dve.reciprocal(gate[:, :], gate_d[:, :]).then_inc(S["gate_inv"], 1)
                dve.wait_ge(S["gate_inv"], n + 1)
                dve.wait_ge(S["vps2"], n + 1)
                dve.wait_ge(S["z2_ready"], n)
                dve.tensor_tensor(gated[:, :], rv, gate[:, :], ALU.mult).then_inc(S["gated_done"], 1)
                dve.wait_ge(S["z2_ready"], n + 1)
                for j in range(NB):
                    dve.bn_stats(stats[:, bass.ds(n * NB + j, 1), :].rearrange("p a k -> p (a k)"),
                                 z_all[:, bass.ds(n * NB + j, 1), :].rearrange("p a d -> p (a d)")).then_inc(S["z2_stats"], 1)

            pairs(dve, mix)
            dve.wait_ge(S["z2_stats"], B * NB)
            norms(2)
            with dve.Fori(0, B) as b:
                for j in range(NB):
                    last = normalise(b, j, z_all[:, bass.ds(b * NB + j, 1), :].rearrange("p a d -> p (a d)"))
                last.then_inc(S["out_ready"], 1)

        @block.gpsimd
        def _(pool):
            def wait(semaphore, value):
                pool.wait_ge(semaphore, value)
                pool.nop(nofuse=True)

            def rotate(n, i, s, more):
                for u in range(2):
                    pool.wait_ge(mul_of[2 * u], n + 1)
                    pool.wait_ge(mul_of[2 * u + 1], n + 1)
                    pool.wait_ge(rest_done[u], n)
                    pool.tensor_tensor(rot[:, u, :], rot_a[:, u, :], rot_b[:, u, :], ALU.add).then_inc(rot_done[u], 1)
                for u in range(2):
                    pool.wait_ge(mid_done[u], n + 1)
                    pool.tensor_tensor(split[:, u, s, 2], rest[:, u, :], split[:, u, s, 1], ALU.subtract).then_inc(lo_done[u], 1)

            pairs(pool, rotate)
            pool.wait_ge(S["v_ready"], B)
            pool.wait_ge(S["fills"], 4)

            def step(b, c):
                new, maxed, scored = (ahead(b, c, k) for k in (4, 3, 2))
                if new:
                    n, bb, cc = new
                    if not (isinstance(n, int) and n < 4):
                        wait(S["av_done"], n - 3)
                    src = v_all[:, bass.ds(bb * NB, NB), 32 * cc:32 * cc + 32].rearrange("p j (g d) -> p j g d", g=G)
                    pool.tensor_copy(vs[:, cc, :, :, 0:HD], src).then_inc(S["v_slot"], 1)
                if maxed:
                    n, bb, cc = maxed
                    nm, rest_, parts = nmax[:, cc % 2, :], nmax_rest[:, :], nsplit[:, cc % 2, :]
                    wait(S["p1_reduced"], 6 * n + 6)
                    if not (isinstance(n, int) and n < 2):
                        wait(S["mt_ps"], n - 1)
                    pool.tensor_copy(parts[:, 0:16], nm).then_inc(S["ns_chain"], 1)
                    pool.wait_ge(S["ns_chain"], 3 * n + 1)
                    pool.tensor_tensor(rest_, nm, parts[:, 0:16], ALU.subtract).then_inc(S["ns_chain"], 1)
                    wait(S["ns_chain"], 3 * n + 2)
                    pool.tensor_copy(parts[:, 16:32], rest_).then_inc(S["ns_chain"], 1)
                    pool.wait_ge(S["ns_chain"], 3 * n + 3)
                    pool.tensor_tensor(parts[:, 32:48], rest_, parts[:, 16:32], ALU.subtract).then_inc(S["ns_ready"], 1)
                if scored:
                    n, bb, cc = scored
                    def keep_causal(view):
                        pool.affine_select(out=view, in_=view, compare_op=ALU.is_ge, fill=0.0, base=0,
                                           pattern=[[0, view.shape[1]], [1, 128]],
                                           channel_multiplier=-1).then_inc(S["mask_done"], 1)
                    wait(S["exp_done"], 10 * n + 8)
                    keep_causal(probs[:, cc % 2, 0:8, 0:128])
                    keep_causal(probs[:, cc % 2, 4:8, 384:512])
                    wait(S["exp_done"], 10 * n + 10)
                    keep_causal(probs[:, cc % 2, 8:10, :].rearrange("p t (k q) -> p (t k) q", k=2)[:, :, 0:128])

            groups(pool, step)

            def mix(n, i, s, more):
                pool.wait_ge(S["x1t_ready"], n + 1)
                wait(S["mix_k"], n)
                pool.tensor_scalar(scaled[:, 1, :], x1_t[:, s, 1:T + 1], mu[:, 1:2], None, ALU.mult).then_inc(S["scaled_k"], 1)
                pool.wait_ge(S["relu_done"], n + 1)
                if not (isinstance(n, int) and n < 2):
                    pool.wait_ge(S["vps2"], n - 1)
                pool.tensor_tensor(k_sq[:, s, :], k_relu[:, :], k_relu[:, :], ALU.mult).then_inc(S["sq_done"], 1)
                pool.wait_ge(S["gated_done"], n + 1)
                pool.tensor_tensor(z_all[:, bass.ds(n * NB, NB), :].rearrange("p i d -> p (i d)"), gated[:, :],
                                   x1[:, s].rearrange("p i d -> p (i d)"), ALU.add).then_inc(S["z2_ready"], 1)

            pairs(pool, mix)


def shape_constants():
    import numpy as np
    freqs = np.float32(1.0) / np.float32(10000.0) ** (np.arange(0, HD, 2, dtype=np.float32) / np.float32(HD))
    angles = np.outer(np.arange(T, dtype=np.float32), freqs.astype(np.float32)).astype(np.float32)
    d_of_row = np.arange(128) // G % HD
    cos = np.cos(angles).T[d_of_row // 2]
    sin = np.sin(angles).T[d_of_row // 2] * np.where(d_of_row % 2, 1.0, -1.0)[:, None]
    eye = np.eye(128)
    causal = np.triu(np.full((128, 128), NEG), 1)
    return {n: np.ascontiguousarray(a, dtype=np.float32)
            for n, a in (("rope_cos", cos), ("rope_sin", sin), ("eye", eye), ("causal", causal))}


def kernel(L0_attn_x, L0_attn_W_qkv, L0_attn_W_out, L0_ffn_W_r, L0_ffn_W_k, L0_ffn_W_v, L0_ffn_mu_r, L0_ffn_mu_k):
    import numpy as _np
    import concourse.bacc as _bacc
    from concourse import mybir as _mybir
    from concourse.bass_utils import run_bass_kernel_spmd as _run

    nc = _bacc.Bacc("TRN2", target_bir_lowering=False, num_devices=1)
    arrays, args = {}, []
    given = [("x", L0_attn_x), ("w_qkv", L0_attn_W_qkv), ("w_out", L0_attn_W_out), ("w_r", L0_ffn_W_r),
             ("w_k", L0_ffn_W_k), ("w_v", L0_ffn_W_v), ("mu_r", L0_ffn_mu_r), ("mu_k", L0_ffn_mu_k)]
    for name, a in given + list(shape_constants().items()):
        a = _np.ascontiguousarray(a)
        arrays[f"in_{name}"] = a
        args.append(nc.dram_tensor(f"in_{name}", a.shape, _mybir.dt.from_np(a.dtype), kind="ExternalInput").ap())
    for name in ("q_parts", "k_parts"):
        args.append(nc.dram_tensor(name, (B, NG, PARTS, 32, T), _mybir.dt.bfloat16, kind="Internal").ap())
    args.append(nc.dram_tensor("out_0", (B, T, D), _mybir.dt.float32, kind="ExternalOutput").ap())
    attention_block(nc, *args)
    r = _run(nc, [arrays], core_ids=[0])
    return r.results[0]["out_0"]
```

```python
import concourse.bass as bass
from concourse import mybir
from contextlib import ExitStack

B, T, D = 8, 512, 128
H, HD = 16, 8
G = 4
NG = H // G
NB = T // 128
NN = B * NG
PARTS = 3
KR = PARTS * PARTS * HD
KM = KR + PARTS
VW = 32
EPS = 1e-5
NEG = -3.0e38
SCALE = float(HD) ** -0.5
TWO_ONES = 1.0019378662109375


def attention_block(nc, x, x_t, w_q, w_k, w_v, w_out, w_ffn, mu_r, mu_k, rope_cos, rope_sin, eye, causal,
                    q_parts, k_parts, out):
    f32 = mybir.dt.float32
    bf16 = mybir.dt.bfloat16
    ALU = mybir.AluOpType
    ACT = mybir.ActivationFunctionType
    AX = mybir.AxisListType

    out_rows = out.rearrange("b (i p) d -> b p i d", p=128)

    ctx = ExitStack()
    with ctx:
        def sb(name, shape, dt=f32):
            return ctx.enter_context(nc.sbuf_tensor(name, shape, dt))

        def sem(name):
            return ctx.enter_context(nc.semaphore(name))

        ident = sb("ident", [128, 128])
        ident_b = sb("ident_b", [128, 128], bf16)
        mask = sb("mask", [128, 128])
        mask_b = sb("mask_b", [128, 128], bf16)
        cos = sb("cos", [128, T])
        sin = sb("sin", [128, T])
        wq_t = sb("wq_t", [128, 2, 128])
        wk_t = sb("wk_t", [128, 2, 128])
        wv_t = sb("wv_t", [128, 128])
        wo_t = sb("wo_t", [128, 128])
        ffn_t = sb("ffn_t", [128, 3, 128])
        mu = sb("mu", [128, 2])
        mu_rest = sb("mu_rest", [128, 2])
        z_all = sb("z_all", [128, B * NB, 128])
        v_all = sb("v_all", [128, B * NB, 128])
        stats = sb("stats", [128, B * NB, 6])
        mean = sb("mean", [128, B * NB])
        rstd = sb("rstd", [128, B * NB])
        half = sb("half", [128, B * NB])
        var = sb("var", [128, B * NB])
        std = sb("std", [128, B * NB])
        shift = sb("shift", [128, B * NB])
        xt = sb("xt", [128, 2, T])
        rot_a = sb("rot_a", [128, 2, T])
        rot_b = sb("rot_b", [128, 2, T])
        rot = sb("rot", [128, 2, 2, T])
        rest = sb("rest", [128, 2, T])
        split = sb("split", [128, 2, 2, PARTS, T], bf16)
        qa = sb("qa", [KM, NG, G * T], bf16)
        ka = sb("ka", [KM, NG, G * T], bf16)
        vs = sb("vs", [128, NG, NB, G, VW])
        probs = sb("probs", [128, 2, 10, 512])
        nmax = sb("nmax", [128, 2, G * NB])
        nmax_rest = sb("nmax_rest", [128, G * NB])
        nsplit = sb("nsplit", [128, 2, 128], bf16)
        nmax_t = sb("nmax_t", [PARTS * G * NB, 2, 128], bf16)
        o_raw = sb("o_raw", [128, T])
        den_inv = sb("den_inv", [128, NB, G])
        o_tok = sb("o_tok", [128, NB, H, HD])
        o_t = sb("o_t", [128, T])
        x1 = sb("x1", [128, 2, NB, 128])
        x1_t = sb("x1_t", [128, 2, T + 1])
        scaled = sb("scaled", [128, 2, T])
        mixed = sb("mixed", [128, 2, 2, T])
        k_relu = sb("k_relu", [128, 2, T])
        k_sq = sb("k_sq", [128, 2, T])
        gate = sb("gate", [128, 2, T])
        gated = sb("gated", [128, T])

        bank = [ctx.enter_context(nc.psum_tensor(f"bank{i}", [128, 512], f32)) for i in range(2)]
        wide = [ctx.enter_context(nc.psum_tensor(f"wide{i}", [128, 1024], f32)) for i in range(2)]
        ps_o = ctx.enter_context(nc.psum_tensor("ps_o", [128, 512], f32))
        ps_m = ctx.enter_context(nc.psum_tensor("ps_m", [128, 512], f32))
        ps_qk = [wide[0][:, 0:512], wide[0][:, 512:1024], wide[1][:, 0:512], wide[1][:, 512:1024]]
        ps_v = [ps_o, ps_m]
        ps_x1t, ps_fv = bank, [ps_o, ps_m]
        ps_k, ps_r = [wide[s][:, 0:512] for s in range(2)], [wide[s][:, 512:1024] for s in range(2)]

        S = {n: sem(n) for n in (
            "weights_in late_weights_in consts_in rope_in z_in mu_in fills ka_ones ident_cast mu_ready "
            "q_mul qs_mul k_mul ks_mul q_ps qs_ps k_ps ks_ps v_ps v_ready "
            "p1_ready p1_reduced ns_chain ns_ready mt_ps mt_ready "
            "p2_ready exp_done v_slot mask_done av_done o_ready ot_raw_ps den_ready o_normed "
            "otok_ps ot_ready y_ps z_ready z_stats "
            "norm_chain var_ready std_ready norm_ready x1_ready x1_kept x1_ps x1t_ready scaled "
            "mix_r mix_k fk_ps r_ps relu_done sq_done gate_ready fv_ps gated_done z2_ready "
            "z2_stats shift_ready out_ready out_ready_act out_scaled out_ready_pool stored").split()}
        xt_ld = [sem(f"xt_ld{s}") for s in range(2)]
        rot_done = [sem(f"rot_done_{u}") for u in "qk"]
        hi_done = [sem(f"hi_done_{u}") for u in "qk"]
        rest_done = [sem(f"rest_done_{u}") for u in "qk"]
        mid_done = [sem(f"mid_done_{u}") for u in "qk"]
        lo_done = [sem(f"lo_done_{u}") for u in "qk"]
        parked = [[sem(f"parked_{u}{s}") for s in range(2)] for u in "qk"]
        qk_ld = [sem(f"qk_ld{c}") for c in range(NG)]
        max_ld = [sem(f"max_ld{c}") for c in range(NG)]

        block = ctx.enter_context(nc.Block())

        mul_of = [S["q_mul"], S["qs_mul"], S["k_mul"], S["ks_mul"]]
        ps_of = [S["q_ps"], S["qs_ps"], S["k_ps"], S["ks_ps"]]

        def turns(eng, turn, lead):
            first = 1 if lead < 3 else 0
            last = (B - lead) // 2 if lead >= 3 else B // 2 - 1
            for m in range(-lead, 2 * first):
                turn(m, m // 2, m % 2)
            with eng.Fori(first, last) as i:
                for s in range(2):
                    turn(2 * i + s, i, s)
            for m in range(2 * last, B):
                turn(m, m // 2, m % 2)

        def batch(m, i, s, lead):
            n = m + lead
            if isinstance(n, int) and not 0 <= n < B:
                return None
            return n, i + (s + lead) // 2, (s + lead) % 2

        def after(eng, semaphore, value):
            if not (isinstance(value, int) and value <= 0):
                eng.wait_ge(semaphore, value)

        def groups(eng, step):
            for b in (-1, 0):
                for c in range(NG):
                    step(b, c)
            with eng.Fori(1, B - 1) as b:
                for c in range(NG):
                    step(b, c)
            for c in range(NG):
                step(B - 1, c)

        def ahead(b, c, lead):
            bb, cc = b + (c + lead) // NG, (c + lead) % NG
            n = NG * bb + cc
            if isinstance(n, int) and not 0 <= n < NN:
                return None
            return n, bb, cc

        PARK = (32, 16)
        LOAD = 16 * 2 * PARTS

        P1 = [(3, 0, 2, 1), (3, 2, 2, 1), (2, 0, 2, 1), (2, 2, 2, 1), (1, 0, 4, 2), (0, 0, 4, 4)]

        @block.sync
        def _(sp):
            sp.dma_start(wq_t[:, :, :], w_q).then_inc(S["weights_in"], 16)
            sp.dma_start(xt[:, 0, :], x_t[:, 0:T]).then_inc(xt_ld[0], 16)
            sp.dma_start(wk_t[:, :, :], w_k).then_inc(S["weights_in"], 16)
            sp.dma_start(wv_t[:, :], w_v).then_inc(S["weights_in"], 16)
            sp.dma_start(cos[:, :], rope_cos).then_inc(S["rope_in"], 16)
            sp.dma_start(sin[:, :], rope_sin).then_inc(S["rope_in"], 16)
            sp.dma_start(xt[:, 1, :], x_t[:, T:2 * T]).then_inc(xt_ld[1], 16)
            sp.dma_start(ident[:, :], eye).then_inc(S["consts_in"], 16)
            sp.dma_start(mask[:, :], causal).then_inc(S["consts_in"], 16)
            sp.dma_start(wo_t[:, :], w_out).then_inc(S["late_weights_in"], 16)
            sp.dma_start(ffn_t[:, :, :], w_ffn).then_inc(S["late_weights_in"], 16)
            sp.dma_start(mu[:, 0:1], mu_r.rearrange("(p a) -> p a", a=1)).then_inc(S["mu_in"], 16)
            sp.dma_start(mu[:, 1:2], mu_k.rearrange("(p a) -> p a", a=1)).then_inc(S["mu_in"], 16)
            sp.dma_start(z_all[:, :, :], x.rearrange("b (i p) d -> p (b i) d", p=128)).then_inc(S["z_in"], 16)

            def load(n, bb, cc):
                def rows(parts, lo):
                    return parts[bb, lo:lo + PARTS, 32 * cc:32 * cc + 32].rearrange("a (d g) t -> a d (g t)", g=G)
                for r in range(PARTS):
                    sp.dma_start(ka[24 * r:24 * r + 24, cc, :], rows(k_parts, 0)).then_inc(qk_ld[cc], 16)
                    sp.dma_start(qa[24 * r:24 * r + 24, cc, :], rows(q_parts, r)).then_inc(qk_ld[cc], 16)

            def park(m, i, s):
                done, far = batch(m, i, s, 0), batch(m, i, s, 2)
                if done and far:
                    n, ii, ss = far
                    sp.wait_ge(S["v_ps"], n - 1)
                    sp.dma_start(xt[:, ss, :], x_t[:, bass.ds(n * T, T)]).then_inc(xt_ld[ss], 16)
                if isinstance(m, int) and m >= B - 2:
                    if m == B - 2:
                        sp.wait_ge(S["ka_ones"], 1)
                        for u in range(2):
                            sp.wait_ge(parked[u][0], PARK[u])
                    for cc in range(2):
                        load(2 * (m - B + 2) + cc, 0, 2 * (m - B + 2) + cc)
                if done:
                    n, ii, ss = done
                    sp.wait_ge(lo_done[0], n + 1)
                    sp.dma_start(q_parts[n, 0:PARTS].rearrange("a p t -> p a t"),
                                 split[:, 0, ss]).then_inc(parked[0][ss], 16)
                    sp.dma_start(q_parts[n, PARTS:].rearrange("a p t -> p a t"),
                                 split[:, 0, ss, 0:PARTS - 1]).then_inc(parked[0][ss], 16)
                    sp.wait_ge(lo_done[1], n + 1)
                    sp.dma_start(k_parts[n].rearrange("a p t -> p a t"), split[:, 1, ss]).then_inc(parked[1][ss], 16)

            turns(sp, park, 1)
            def feed(b, c):
                g = ahead(b, c, 4)
                if g and not (isinstance(b, int) and b < 0):
                    if isinstance(b, int) and g[0] == NG:
                        for u in range(2):
                            for s in range(2):
                                sp.wait_ge(parked[u][s], PARK[u] * (B // 2))
                    sp.wait_ge(S["p2_ready"], 10 * (g[0] - 3))
                    load(*g)

            groups(sp, feed)

            with sp.Fori(0, B) as b:
                sp.wait_ge(S["out_ready"], b + 1)
                sp.wait_ge(S["out_ready_act"], b + 1)
                sp.wait_ge(S["out_ready_pool"], b + 1)
                sp.dma_start(out_rows[b], z_all[:, bass.ds(b * NB, NB), :]).then_inc(S["stored"], 16)
            sp.wait_ge(S["stored"], 16 * B)

        @block.tensor
        def _(pe):
            pe.wait_ge(S["weights_in"], 16 * 3)

            def project(m, i, s):
                new = batch(m, i, s, 1)
                if not new:
                    return
                n, ii, ss = new
                pe.wait_ge(xt_ld[ss], 16 * (ii + 1))
                for a, w in enumerate((wq_t[:, 0, :], wq_t[:, 1, :], wk_t[:, 0, :], wk_t[:, 1, :])):
                    after(pe, mul_of[a], n)
                    pe.matmul(ps_qk[a], w, xt[:, ss, :], start=True, stop=True).then_inc(ps_of[a], 1)
                after(pe, S["v_ready"], n - 1)
                for j in range(NB):
                    mm = pe.matmul(ps_v[ss][:, 128 * j:128 * j + 128], xt[:, ss, 128 * j:128 * j + 128],
                                   wv_t[:, :], start=True, stop=True)
                mm.then_inc(S["v_ps"], 1)

            turns(pe, project, 1)

            for m in mul_of:
                pe.wait_ge(m, B)
            pe.wait_ge(S["v_ready"], B)
            pe.wait_ge(S["ident_cast"], 2)
            pe.wait_ge(S["late_weights_in"], 32)

            def p1_tile(g, t):
                n, bb, cc = g
                if t == 0:
                    pe.wait_ge(qk_ld[cc], LOAD * (bb + 1))
                if not (isinstance(n, int) and n == 0 and t < 2):
                    pe.wait_ge(S["p1_reduced"], 6 * n + t - 1)
                i, g0, heads, per = P1[t]
                keys = 128 * (i + 1)
                for h in range(heads):
                    at = 512 * (h // per) + keys * (h % per)
                    tok = T * (g0 + h)
                    pe.matmul(wide[t % 2][:, at:at + keys], qa[0:KR, cc, tok + 128 * i:tok + keys],
                              ka[0:KR, cc, tok:tok + keys], start=True, stop=False)
                    mm = pe.matmul(wide[t % 2][:, at + keys - 128:at + keys], ident_b[:, :], mask_b[:, :],
                                   start=False, stop=True)
                mm.then_inc(S["p1_ready"], 1)

            def p2_tile(g, t):
                n, bb, cc = g
                if t == 0:
                    pe.wait_ge(max_ld[cc], 16 * (bb + 1))
                if not (isinstance(n, int) and n == 0 and t < 2):
                    pe.wait_ge(S["exp_done"], 10 * n + t - 1)

                def block_of(h, j, at):
                    tok = T * h
                    return pe.matmul(bank[t % 2][:, at:at + T - 128 * j],
                                     ka[0:KM, cc, tok + 128 * j:tok + 128 * j + 128],
                                     qa[0:KM, cc, tok + 128 * j:tok + T], start=True, stop=True)
                if t < 4:
                    mm = block_of(t, 0, 0)
                elif t < 8:
                    block_of(t - 4, 1, 0)
                    mm = block_of(t - 4, 3, 384)
                else:
                    block_of(2 * (t - 8), 2, 0)
                    mm = block_of(2 * (t - 8) + 1, 2, 256)
                mm.then_inc(S["p2_ready"], 1)

            def p_block(par, h, j):
                if j == 0:
                    return probs[:, par, h, :]
                if j == 1:
                    return probs[:, par, 4 + h, 0:384]
                if j == 3:
                    return probs[:, par, 4 + h, 384:512]
                return probs[:, par, 8 + h // 2, 256 * (h % 2):256 * (h % 2) + 256]

            def av(g, j):
                n, bb, cc = g
                pe.wait_ge(S["mask_done"], 3 * n + (1, 1, 3, 2)[j])
                if j == 0:
                    pe.wait_ge(S["v_slot"], n + 1)
                    pe.wait_ge(S["o_ready"], n)
                for h in range(G):
                    mm = pe.matmul(ps_o[32 * h:32 * h + 32, 128 * j:T], vs[:, cc, j, h, :],
                                   p_block(cc % 2, h, j), start=(j == 0), stop=(j == 2))
                if j == 2:
                    mm.then_inc(S["av_done"], 1)

            def max_transpose(g):
                n, bb, cc = g
                pe.wait_ge(S["ns_ready"], n + 1)
                pe.transpose(ps_m[:, 0:64].bitcast(bf16), nsplit[:, cc % 2, :], ident_b[:, :]).then_inc(S["mt_ps"], 1)

            def o_transposes(g):
                n, bb, cc = g
                pe.wait_ge(S["o_ready"], n + 1)
                for j in range(NB):
                    mm = pe.transpose(ps_m[:, 128 * j:128 * j + 128], o_raw[:, 128 * j:128 * j + 128], ident[:, :])
                mm.then_inc(S["ot_raw_ps"], 1)

            def step(b, c):
                new, scored, mult, maxed, post = (ahead(b, c, k) for k in (4, 2, 1, 3, 0))

                def p1(t):
                    if new:
                        p1_tile(new, t)

                def p2(t):
                    if scored:
                        p2_tile(scored, t)

                def pv(j):
                    if mult:
                        av(mult, j)

                def max_part():
                    if maxed:
                        if post:
                            after(pe, S["o_normed"], post[0])
                            if c == 0:
                                after(pe, S["z_ready"], post[1])
                        max_transpose(maxed)

                def post_part():
                    if post:
                        if maxed:
                            pe.wait_ge(S["mt_ready"], maxed[0] + 1)
                        else:
                            pe.wait_ge(S["o_normed"], post[0])
                        o_transposes(post)

                def batch_transposes():
                    pe.wait_ge(S["o_normed"], post[0] + 1)
                    for j in range(NB):
                        mm = pe.transpose(ps_m[:, 128 * j:128 * j + 128],
                                          o_tok[:, j].rearrange("p h d -> p (h d)"), ident[:, :])
                    mm.then_inc(S["otok_ps"], 1)

                def batch_projection():
                    pe.wait_ge(S["ot_ready"], post[1] + 1)
                    for j in range(NB):
                        mm = pe.matmul(ps_m[:, 128 * j:128 * j + 128], o_t[:, 128 * j:128 * j + 128],
                                       wo_t[:, :], start=True, stop=True)
                    mm.then_inc(S["y_ps"], 1)

                whole = post and c == NG - 1
                p2(0)
                p1(0)
                p2(1)
                p1(1)
                pv(0)
                p2(2)
                p2(3)
                pv(1)
                max_part()
                p1(2)
                p2(4)
                p2(5)
                p1(3)
                pv(3)
                post_part()
                p2(6)
                p1(4)
                p2(7)
                if whole:
                    batch_transposes()
                pv(2)
                p2(8)
                p1(5)
                p2(9)
                if whole:
                    batch_projection()

            groups(pe, step)

            pe.wait_ge(S["z_ready"], B)

            def channel_mix(m, i, s):
                new, mid, old = (batch(m, i, s, k) for k in (2, 1, 0))
                if mid:
                    n, _, ss = mid
                    pe.wait_ge(S["mix_k"], n + 1)
                    after(pe, S["relu_done"], n - 1)
                    pe.matmul(ps_k[ss], ffn_t[:, 1, :], mixed[:, ss, 1, :], start=True, stop=True).then_inc(S["fk_ps"], 1)
                if new:
                    n, _, ss = new
                    pe.wait_ge(S["x1_ready"], n + 1)
                    after(pe, S["x1t_ready"], n - 1)
                    for j in range(NB):
                        mm = pe.transpose(ps_x1t[ss][:, 128 * j:128 * j + 128], x1[:, ss, j, :], ident[:, :])
                    mm.then_inc(S["x1_ps"], 1)
                if old:
                    n, _, ss = old
                    pe.wait_ge(S["sq_done"], n + 1)
                    after(pe, S["gated_done"], n - 1)
                    for j in range(NB):
                        mm = pe.matmul(ps_fv[ss][:, 128 * j:128 * j + 128], k_sq[:, ss, 128 * j:128 * j + 128],
                                       ffn_t[:, 2, :], start=True, stop=True)
                    mm.then_inc(S["fv_ps"], 1)
                if mid:
                    n, _, ss = mid
                    pe.wait_ge(S["mix_r"], n + 1)
                    after(pe, S["gate_ready"], n - 1)
                    for j in range(NB):
                        mm = pe.matmul(ps_r[ss][:, 128 * j:128 * j + 128], mixed[:, ss, 0, 128 * j:128 * j + 128],
                                       ffn_t[:, 0, :], start=True, stop=True)
                    mm.then_inc(S["r_ps"], 1)

            turns(pe, channel_mix, 2)

        @block.scalar
        def _(act):
            def copy(dst, src):
                return act.activation(dst, src, ACT.Copy)

            def split_parts(m, i, s):
                n, ii, ss = batch(m, i, s, 0)

                def first(u):
                    act.wait_ge(rot_done[u], n + 1)
                    after(act, parked[u][ss], PARK[u] * ii)
                    copy(split[:, u, ss, 0], rot[:, ss, u, :]).then_inc(hi_done[u], 1)

                def second(u):
                    act.wait_ge(rest_done[u], n + 1)
                    copy(split[:, u, ss, 1], rest[:, u, :]).then_inc(mid_done[u], 1)

                first(0)
                second(0)
                first(1)
                act.wait_ge(S["v_ps"], n + 1)
                copy(v_all[:, bass.ds(n * NB, NB), :].rearrange("p i d -> p (i d)"), ps_v[ss][:, :]).then_inc(S["v_ready"], 1)
                second(1)

            turns(act, split_parts, 0)

            def step(b, c):
                maxed, scored, mult, post = (ahead(b, c, k) for k in (3, 2, 1, 0))

                def exps(t0, t1):
                    if not scored:
                        return
                    n, bb, cc = scored
                    for t in range(t0, t1):
                        if t == 0 and not (isinstance(n, int) and n < 2):
                            act.wait_ge(S["av_done"], n - 1)
                        act.wait_ge(S["p2_ready"], 10 * n + t + 1)
                        act.activation(probs[:, cc % 2, t, :], bank[t % 2][:, :], ACT.Exp,
                                       scale=SCALE).then_inc(S["exp_done"], 1)

                exps(0, 6)
                if maxed:
                    n, bb, cc = maxed
                    act.wait_ge(S["mt_ready"], n + 1)
                    act.dma_start(qa[KR:KM, cc, :].rearrange("a (x q) -> a x q", q=128),
                                  nmax_t[:, cc % 2, :]).then_inc(max_ld[cc], 16)
                exps(6, 8)
                if post and c == NG - 1:
                    act.wait_ge(S["otok_ps"], post[1] + 1)
                    act.wait_ge(S["y_ps"], post[1])
                    copy(o_t[:, :], ps_m[:, :]).then_inc(S["ot_ready"], 1)
                exps(8, 10)
                if mult:
                    n = mult[0]
                    act.wait_ge(S["av_done"], n + 1)
                    act.wait_ge(S["ot_raw_ps"], n)
                    copy(o_raw[:, :], ps_o[:, :]).then_inc(S["o_ready"], 1)

            groups(act, step)

            def root(k):
                act.wait_ge(S["var_ready"], k)
                act.activation(std[:, :], var[:, :], ACT.Sqrt).then_inc(S["std_ready"], 1)

            root(1)

            act.wait_ge(S["mu_in"], 32)

            def mix(m, i, s):
                new, mid = (batch(m, i, s, k) for k in (2, 1))
                if mid:
                    n, _, ss = mid
                    act.wait_ge(S["fk_ps"], n + 1)
                    after(act, S["sq_done"], n - 1)
                    act.activation(k_relu[:, ss, :], ps_k[ss], ACT.Relu).then_inc(S["relu_done"], 1)
                if new:
                    n, _, ss = new
                    act.wait_ge(S["x1_ps"], n + 1)
                    after(act, S["mix_r"], n - 1)
                    copy(x1_t[:, ss, 1:T + 1], ps_x1t[ss][:, :]).then_inc(S["x1t_ready"], 1)
                    act.wait_ge(S["x1t_ready"], n + 1)
                    for a, name in ((1, "mix_k"), (0, "mix_r")):
                        after(act, S[name], n)
                        act.activation(scaled[:, a, :], x1_t[:, ss, 1:T + 1], ACT.Copy,
                                       scale=mu[:, a:a + 1]).then_inc(S["scaled"], 1)
                if mid:
                    n, _, ss = mid
                    act.wait_ge(S["r_ps"], n + 1)
                    after(act, S["gated_done"], n - 1)
                    act.activation(gate[:, ss, :], ps_r[ss], ACT.Sigmoid).then_inc(S["gate_ready"], 1)

            turns(act, mix, 2)
            root(2)
            act.wait_ge(S["shift_ready"], 1)
            with act.Fori(0, B) as b:
                at = b * NB + 2
                z = z_all[:, bass.ds(at, 1), :].rearrange("p a d -> p (a d)")
                act.activation(z, z, ACT.Identity, scale=rstd[:, bass.ds(at, 1)],
                               bias=shift[:, bass.ds(at, 1)]).then_inc(S["out_ready_act"], 1)

        @block.vector
        def _(dve):
            dve.memset(vs[:, :, :, :, :], 1.0).then_inc(S["fills"], 1)
            dve.memset(x1_t[:, :, 0:1], 0.0).then_inc(S["fills"], 1)
            dve.memset(nsplit[:, :, :], 0.0).then_inc(S["fills"], 1)
            dve.wait_ge(S["rope_in"], 32)

            def rotate(m, i, s):
                new, old = batch(m, i, s, 1), batch(m, i, s, 0)
                for u in range(2):
                    if old:
                        n, _, ss = old
                        dve.wait_ge(hi_done[u], n + 1)
                        after(dve, lo_done[u], n)
                        dve.tensor_tensor(rest[:, u, :], rot[:, ss, u, :], split[:, u, ss, 0], ALU.subtract).then_inc(rest_done[u], 1)
                    if new:
                        n = new[0]
                        for a in (2 * u, 2 * u + 1):
                            dve.wait_ge(ps_of[a], n + 1)
                            after(dve, rot_done[u], n)
                            dst, table = ((rot_a, cos), (rot_b, sin))[a % 2]
                            dve.tensor_tensor(dst[:, u, :], ps_qk[a], table[:, :], ALU.mult).then_inc(mul_of[a], 1)

            turns(dve, rotate, 1)
            dve.wait_ge(S["consts_in"], 32)
            dve.tensor_copy(ident_b[:, :], ident[:, :]).then_inc(S["ident_cast"], 1)
            dve.tensor_copy(mask_b[:, :], mask[:, :]).then_inc(S["ident_cast"], 1)
            dve.wait_ge(S["mu_in"], 32)
            dve.tensor_scalar(mu_rest[:, :], mu[:, :], -1.0, 1.0, ALU.mult, ALU.add).then_inc(S["mu_ready"], 1)

            def step(b, c):
                new, maxed, post = (ahead(b, c, k) for k in (4, 3, 0))

                def reduce(t):
                    if not new:
                        return
                    n, bb, cc = new
                    if t == 0 and not (isinstance(n, int) and n < 2):
                        dve.wait_ge(S["ns_ready"], n - 1)
                    dve.wait_ge(S["p1_ready"], 6 * n + t + 1)
                    i, g0, heads, per = P1[t]
                    keys = 128 * (i + 1)
                    src = wide[t % 2][:, 0:512 * (heads // per)].rearrange("p (k n) -> p k n", n=512)[:, :, 0:keys * per]
                    dst = nmax[:, cc % 2, :].rearrange("p (g i) -> p g i", i=NB)[:, g0:g0 + heads, i]
                    if per > 1:
                        src = wide[t % 2][:, 0:keys * heads].rearrange("p (h m) -> p h m", m=keys)
                    dve.tensor_reduce(dst, src, AX.X, ALU.max, negate=True).then_inc(S["p1_reduced"], 1)

                reduce(0)
                reduce(1)
                if maxed:
                    n, bb, cc = maxed
                    dve.wait_ge(S["mt_ps"], n + 1)
                    if not (isinstance(n, int) and n < 2):
                        b2, c2 = bb + (cc - 2) // NG, (cc - 2) % NG
                        dve.wait_ge(max_ld[c2], 16 * (b2 + 1))
                    dve.tensor_copy(nmax_t[:, cc % 2, :], ps_m[0:PARTS * G * NB, 0:64].bitcast(bf16)).then_inc(S["mt_ready"], 1)
                reduce(2)
                reduce(3)
                if post:
                    n, bb, cc = post
                    o = ps_m[:, :].rearrange("p (j g w) -> p j g w", j=NB, g=G)
                    dve.wait_ge(S["ot_raw_ps"], n + 1)
                    dve.wait_ge(S["o_normed"], n)
                    dve.wait_ge(S["otok_ps"], bb)
                    dve.reciprocal(den_inv[:, :, :], o[:, :, :, HD]).then_inc(S["den_ready"], 1)
                    dve.wait_ge(S["den_ready"], n + 1)
                    dve.tensor_tensor(o_tok[:, :, G * cc:G * cc + G, :], o[:, :, :, 0:HD],
                                      den_inv[:, :, :].unsqueeze(3).to_broadcast((128, NB, G, HD)), ALU.mult).then_inc(S["o_normed"], 1)
                reduce(4)
                reduce(5)
                if post and c == NG - 1:
                    bb = post[1]
                    if isinstance(bb, int) and bb == 0 or not isinstance(bb, int):
                        dve.wait_ge(S["z_in"], 16)
                    dve.wait_ge(S["y_ps"], bb + 1)
                    z = z_all[:, bass.ds(bb * NB, NB), :]
                    dve.tensor_tensor(z, ps_m[:, :].rearrange("p (i d) -> p i d", i=NB), z, ALU.add).then_inc(S["z_ready"], 1)
                    dve.wait_ge(S["z_ready"], bb + 1)
                    for j in range(NB):
                        dve.bn_stats(stats[:, bass.ds(bb * NB + j, 1), :].rearrange("p a k -> p (a k)"),
                                     z_all[:, bass.ds(bb * NB + j, 1), :].rearrange("p a d -> p (a d)")).then_inc(S["z_stats"], 1)

            groups(dve, step)

            chain = [0]

            def link(ins):
                chain[0] += 1
                ins.then_inc(S["norm_chain"], 1)
                dve.wait_ge(S["norm_chain"], chain[0])

            def norms(k):
                m_even, q_even, m_odd, q_odd = (stats[:, :, a] for a in (1, 2, 4, 5))
                link(dve.tensor_tensor(half[:, :], m_even, m_odd, ALU.subtract))
                link(dve.tensor_scalar(half[:, :], half[:, :], 0.5, None, ALU.mult))
                link(dve.tensor_tensor(mean[:, :], half[:, :], m_odd, ALU.add))
                link(dve.tensor_tensor(half[:, :], half[:, :], half[:, :], ALU.mult))
                link(dve.tensor_tensor(var[:, :], q_even, q_odd, ALU.add))
                link(dve.tensor_scalar(var[:, :], var[:, :], 1.0 / D, EPS, ALU.mult, ALU.add))
                dve.tensor_tensor(var[:, :], var[:, :], half[:, :], ALU.add).then_inc(S["var_ready"], 1)
                dve.wait_ge(S["std_ready"], k)
                dve.reciprocal(rstd[:, :], std[:, :]).then_inc(S["norm_ready"], 1)
                dve.wait_ge(S["norm_ready"], k)

            dve.wait_ge(S["z_stats"], B * NB)
            norms(1)

            def normalise(n, j, dst):
                at = n * NB + j
                return dve.tensor_scalar(dst, z_all[:, bass.ds(at, 1), :].rearrange("p a d -> p (a d)"),
                                         mean[:, bass.ds(at, 1)], rstd[:, bass.ds(at, 1)], ALU.subtract, ALU.mult)

            dve.wait_ge(S["mu_ready"], 1)

            def mix(m, i, s):
                new, mid, old, summed = (batch(m, i, s, k) for k in (3, 2, 1, 0))

                def mixed_input(a, name, nth):
                    n, _, ss = mid
                    after(dve, S["r_ps"], n - 1)
                    dve.wait_ge(S["scaled"], 2 * n + nth)
                    dve.scalar_tensor_tensor(out=mixed[:, ss, a, :], in0=x1_t[:, ss, 0:T],
                                             scalar=mu_rest[:, a:a + 1], in1=scaled[:, a, :],
                                             op0=ALU.mult, op1=ALU.add).then_inc(S[name], 1)

                if mid:
                    mixed_input(1, "mix_k", 1)
                if new:
                    n, _, ss = new
                    after(dve, S["x1_kept"], n - 1)
                    after(dve, S["x1_ps"], n - 1)
                    for j in range(NB):
                        last = normalise(n, j, x1[:, ss, j, :])
                    last.then_inc(S["x1_ready"], 1)
                if mid:
                    mixed_input(0, "mix_r", 2)
                if summed:
                    n, _, ss = summed
                    dve.wait_ge(S["z2_ready"], n + 1)
                    for j in range(NB):
                        dve.bn_stats(stats[:, bass.ds(n * NB + j, 1), :].rearrange("p a k -> p (a k)"),
                                     z_all[:, bass.ds(n * NB + j, 1), :].rearrange("p a d -> p (a d)")).then_inc(S["z2_stats"], 1)
                if old:
                    n, _, ss = old
                    dve.wait_ge(S["fv_ps"], n + 1)
                    dve.wait_ge(S["gate_ready"], n + 1)
                    after(dve, S["z2_ready"], n)
                    dve.tensor_tensor(gated[:, :], ps_fv[ss][:, :], gate[:, ss, :], ALU.mult).then_inc(S["gated_done"], 1)

            turns(dve, mix, 3)
            dve.wait_ge(S["z2_stats"], B * NB)
            norms(2)
            link(dve.tensor_tensor(half[:, :], mean[:, :], rstd[:, :], ALU.mult))
            dve.tensor_scalar(shift[:, :], half[:, :], -1.0, None, ALU.mult).then_inc(S["shift_ready"], 1)
            with dve.Fori(0, B) as b:
                for j in range(2):
                    last = normalise(b, j, z_all[:, bass.ds(b * NB + j, 1), :].rearrange("p a d -> p (a d)"))
                last.then_inc(S["out_ready"], 1)

        @block.gpsimd
        def _(pool):
            def wait(semaphore, value):
                pool.wait_ge(semaphore, value)
                pool.nop(nofuse=True)

            pool.memset(ka[64:KM, :, :].bitcast(f32), TWO_ONES).then_inc(S["ka_ones"], 1)
            pool.wait_ge(S["ka_ones"], 1)

            def rotate(m, i, s):
                new, old = batch(m, i, s, 1), batch(m, i, s, 0)
                for u in range(2):
                    if old:
                        n, _, ss = old
                        pool.wait_ge(mid_done[u], n + 1)
                        pool.tensor_tensor(split[:, u, ss, 2], rest[:, u, :], split[:, u, ss, 1], ALU.subtract).then_inc(lo_done[u], 1)
                    if new:
                        n, _, ss = new
                        pool.wait_ge(mul_of[2 * u], n + 1)
                        pool.wait_ge(mul_of[2 * u + 1], n + 1)
                        after(pool, rest_done[u], n - 1)
                        pool.tensor_tensor(rot[:, ss, u, :], rot_a[:, u, :], rot_b[:, u, :], ALU.add).then_inc(rot_done[u], 1)

            turns(pool, rotate, 1)
            pool.wait_ge(S["v_ready"], B)
            pool.wait_ge(S["fills"], 3)

            def step(b, c):
                new, maxed, scored = (ahead(b, c, k) for k in (4, 3, 2))
                if new:
                    n, bb, cc = new
                    if not (isinstance(n, int) and n < 4):
                        wait(S["av_done"], n - 3)
                    src = v_all[:, bass.ds(bb * NB, NB), 32 * cc:32 * cc + 32].rearrange("p j (g d) -> p j g d", g=G)
                    pool.tensor_copy(vs[:, cc, :, :, 0:HD], src).then_inc(S["v_slot"], 1)
                if maxed:
                    n, bb, cc = maxed
                    nm, rest_, parts = nmax[:, cc % 2, :], nmax_rest[:, :], nsplit[:, cc % 2, :]
                    wait(S["p1_reduced"], 6 * n + 6)
                    if not (isinstance(n, int) and n < 2):
                        wait(S["mt_ps"], n - 1)
                    pool.tensor_copy(parts[:, 0:16], nm).then_inc(S["ns_chain"], 1)
                    pool.wait_ge(S["ns_chain"], 3 * n + 1)
                    pool.tensor_tensor(rest_, nm, parts[:, 0:16], ALU.subtract).then_inc(S["ns_chain"], 1)
                    wait(S["ns_chain"], 3 * n + 2)
                    pool.tensor_copy(parts[:, 16:32], rest_).then_inc(S["ns_chain"], 1)
                    pool.wait_ge(S["ns_chain"], 3 * n + 3)
                    pool.tensor_tensor(parts[:, 32:48], rest_, parts[:, 16:32], ALU.subtract).then_inc(S["ns_ready"], 1)
                if scored:
                    n, bb, cc = scored
                    def keep_causal(view):
                        pool.affine_select(out=view, in_=view, compare_op=ALU.is_ge, fill=0.0, base=0,
                                           pattern=[[0, view.shape[1]], [1, 128]],
                                           channel_multiplier=-1).then_inc(S["mask_done"], 1)
                    wait(S["exp_done"], 10 * n + 8)
                    keep_causal(probs[:, cc % 2, 0:8, 0:128])
                    keep_causal(probs[:, cc % 2, 4:8, 384:512])
                    wait(S["exp_done"], 10 * n + 10)
                    keep_causal(probs[:, cc % 2, 8:10, :].rearrange("p t (k q) -> p (t k) q", k=2)[:, :, 0:128])

            groups(pool, step)

            def mix(m, i, s):
                new, mid, old = (batch(m, i, s, k) for k in (2, 1, 0))
                if new:
                    n, _, ss = new
                    wait(S["x1_ready"], n + 1)
                    pool.tensor_copy(z_all[:, bass.ds(n * NB, NB), :].rearrange("p i d -> p (i d)"),
                                     x1[:, ss].rearrange("p i d -> p (i d)")).then_inc(S["x1_kept"], 1)
                if mid:
                    n, _, ss = mid
                    pool.wait_ge(S["relu_done"], n + 1)
                    after(pool, S["fv_ps"], n - 1)
                    pool.tensor_tensor(k_sq[:, ss, :], k_relu[:, ss, :], k_relu[:, ss, :], ALU.mult).then_inc(S["sq_done"], 1)
                if old:
                    n, _, ss = old
                    pool.wait_ge(S["x1_kept"], n + 1)
                    pool.wait_ge(S["gated_done"], n + 1)
                    z = z_all[:, bass.ds(n * NB, NB), :].rearrange("p i d -> p (i d)")
                    pool.tensor_tensor(z, gated[:, :], z, ALU.add).then_inc(S["z2_ready"], 1)

            turns(pool, mix, 2)
            pool.wait_ge(S["shift_ready"], 1)
            with pool.Fori(0, B) as b:
                at = b * NB + 3
                z = z_all[:, bass.ds(at, 1), :].rearrange("p a d -> p (a d)")
                pool.tensor_tensor(z, z, rstd[:, bass.ds(at, 1)].to_broadcast((128, 128)), ALU.mult).then_inc(S["out_scaled"], 1)
                pool.wait_ge(S["out_scaled"], b + 1)
                pool.tensor_tensor(z, z, shift[:, bass.ds(at, 1)].to_broadcast((128, 128)), ALU.add).then_inc(S["out_ready_pool"], 1)


def shape_constants():
    import numpy as np
    freqs = np.float32(1.0) / np.float32(10000.0) ** (np.arange(0, HD, 2, dtype=np.float32) / np.float32(HD))
    angles = np.outer(np.arange(T, dtype=np.float32), freqs.astype(np.float32)).astype(np.float32)
    d_of_row = np.arange(128) // G % HD
    cos = np.cos(angles).T[d_of_row // 2]
    sin = np.sin(angles).T[d_of_row // 2] * np.where(d_of_row % 2, 1.0, -1.0)[:, None]
    eye = np.eye(128)
    causal = np.triu(np.full((128, 128), NEG), 1)
    return {n: np.ascontiguousarray(a, dtype=np.float32)
            for n, a in (("rope_cos", cos), ("rope_sin", sin), ("eye", eye), ("causal", causal))}


def kernel(L0_attn_x, L0_attn_W_qkv, L0_attn_W_out, L0_ffn_W_r, L0_ffn_W_k, L0_ffn_W_v, L0_ffn_mu_r, L0_ffn_mu_k):
    import numpy as _np
    import concourse.bacc as _bacc
    from concourse import mybir as _mybir
    from concourse.bass_utils import run_bass_kernel_spmd as _run

    nc = _bacc.Bacc("TRN2", target_bir_lowering=False, num_devices=1)
    arrays, args = {}, []
    wq, wk, wv = (_np.asarray(L0_attn_W_qkv)[D * a:D * a + D] for a in range(3))
    order = _np.arange(D).reshape(NG, G, HD).transpose(0, 2, 1)
    swapped = order.reshape(NG, HD // 2, 2, G)[:, :, ::-1]
    rows = _np.stack([order.reshape(-1), swapped.reshape(-1)])
    given = [("x", L0_attn_x), ("x_t", _np.asarray(L0_attn_x).reshape(B * T, D).T),
             ("w_q", wq[rows].transpose(2, 0, 1)), ("w_k", wk[rows].transpose(2, 0, 1)), ("w_v", wv.T),
             ("w_out", _np.asarray(L0_attn_W_out).T),
             ("w_ffn", _np.stack([_np.asarray(L0_ffn_W_r).T, _np.asarray(L0_ffn_W_k).T,
                                  _np.asarray(L0_ffn_W_v).T], axis=1)),
             ("mu_r", L0_ffn_mu_r), ("mu_k", L0_ffn_mu_k)]
    for name, a in given + list(shape_constants().items()):
        a = _np.ascontiguousarray(a)
        arrays[f"in_{name}"] = a
        args.append(nc.dram_tensor(f"in_{name}", a.shape, _mybir.dt.from_np(a.dtype), kind="ExternalInput").ap())
    for name, parts in (("q_parts", 2 * PARTS - 1), ("k_parts", PARTS)):
        args.append(nc.dram_tensor(name, (B, parts, 128, T), _mybir.dt.bfloat16, kind="Internal").ap())
    args.append(nc.dram_tensor("out_0", (B, T, D), _mybir.dt.float32, kind="ExternalOutput").ap())
    attention_block(nc, *args)
    r = _run(nc, [arrays], core_ids=[0])
    return r.results[0]["out_0"]
```

```python
import concourse.bass as bass
from concourse import mybir
from contextlib import ExitStack

B, T, D = 8, 512, 128
H, HD = 16, 8
G = 4
NG = H // G
NB = T // 128
NN = B * NG
PARTS = 3
KR = PARTS * PARTS * HD
KM = KR + PARTS
VW = 32
EPS = 1e-5
NEG = -3.0e38
SCALE = float(HD) ** -0.5
TWO_ONES = 1.0019378662109375


def attention_block(nc, x, x_t, w_q, w_k, w_v, w_out, w_ffn, mu_r, mu_k, rope_cos, rope_sin, eye,
                    q_parts, k_parts, out):
    f32 = mybir.dt.float32
    bf16 = mybir.dt.bfloat16
    ALU = mybir.AluOpType
    ACT = mybir.ActivationFunctionType
    AX = mybir.AxisListType

    out_rows = out.rearrange("(n b) (i p) d -> n p (b i) d", b=2, p=128)

    ctx = ExitStack()
    with ctx:
        def sb(name, shape, dt=f32):
            return ctx.enter_context(nc.sbuf_tensor(name, shape, dt))

        def sem(name):
            return ctx.enter_context(nc.semaphore(name))

        ident = sb("ident", [128, 128])
        ident_b = sb("ident_b", [128, 128], bf16)
        cos = sb("cos", [128, T])
        sin = sb("sin", [128, T])
        wq_t = sb("wq_t", [128, 2, 128])
        wk_t = sb("wk_t", [128, 2, 128])
        wv_t = sb("wv_t", [128, 128])
        wo_t = sb("wo_t", [128, 128])
        ffn_t = sb("ffn_t", [128, 3, 128])
        mu = sb("mu", [128, 2])
        mu_rest = sb("mu_rest", [128, 2])
        z_all = sb("z_all", [128, B * NB, 128])
        v_all = sb("v_all", [128, B * NB, 128])
        stats = sb("stats", [128, B * NB, 6])
        mean = sb("mean", [128, B * NB])
        rstd = sb("rstd", [128, B * NB])
        half = sb("half", [128, B * NB])
        var = sb("var", [128, B * NB])
        std = sb("std", [128, B * NB])
        shift = sb("shift", [128, B * NB])
        xt = sb("xt", [128, 2, T])
        rot_a = sb("rot_a", [128, 2, T])
        rot_b = sb("rot_b", [128, 2, T])
        rot = sb("rot", [128, 2, 2, T])
        rest = sb("rest", [128, 2, T])
        split = sb("split", [128, 2, 2, PARTS, T], bf16)
        qa = sb("qa", [KM, NG, G * T], bf16)
        ka = sb("ka", [KM, NG, G * T], bf16)
        vs = sb("vs", [128, NG, NB, G, VW])
        probs = sb("probs", [128, 2, 10, 512])
        diag = sb("diag", [128, 2, 2 * G, 128])
        nbefore = sb("nbefore", [128, G, NB - 1])
        nmax = sb("nmax", [128, 2, G * NB])
        nmax_rest = sb("nmax_rest", [128, G * NB])
        nsplit = sb("nsplit", [128, 2, 128], bf16)
        nmax_t = sb("nmax_t", [PARTS * G * NB, 2, 128], bf16)
        o_raw = sb("o_raw", [128, T])
        den_inv = sb("den_inv", [128, NB, G])
        o_tok = sb("o_tok", [128, NB, H, HD])
        o_t = sb("o_t", [128, T])
        x1 = sb("x1", [128, 2, NB, 128])
        x1_t = sb("x1_t", [128, 2, T + 1])
        scaled = sb("scaled", [128, 2, T])
        mixed = sb("mixed", [128, 2, 2, T])
        k_relu = sb("k_relu", [128, 2, T])
        k_sq = sb("k_sq", [128, 2, T])
        gate = sb("gate", [128, 2, T])
        gated = o_t

        bank = [ctx.enter_context(nc.psum_tensor(f"bank{i}", [128, 512], f32)) for i in range(2)]
        wide = [ctx.enter_context(nc.psum_tensor(f"wide{i}", [128, 1024], f32)) for i in range(2)]
        ps_o = ctx.enter_context(nc.psum_tensor("ps_o", [128, 512], f32))
        ps_m = ctx.enter_context(nc.psum_tensor("ps_m", [128, 512], f32))
        ps_qk = [wide[0][:, 0:512], wide[0][:, 512:1024], wide[1][:, 0:512], wide[1][:, 512:1024]]
        ps_v = [ps_o, ps_m]
        ps_x1t, ps_fv = bank, [ps_o, ps_m]
        ps_k, ps_r = [wide[s][:, 0:512] for s in range(2)], [wide[s][:, 512:1024] for s in range(2)]

        S = {n: sem(n) for n in (
            "w_q_in weights_in late_weights_in consts_in rope_in z_in mu_in fills ka_ones ident_cast mu_ready "
            "q_mul qs_mul k_mul ks_mul q_ps qs_ps k_ps ks_ps v_ps v_ready "
            "diag_ps diag_copied diag_masked diag_reduced p1_ready p1_reduced nmax_ready "
            "ns_chain ns_ready mt_ps mt_ready "
            "p2_ready exp_done v_slot mask_done av_done o_ready ot_raw_ps den_ready o_normed "
            "otok_ps ot_ready y_ps z_ready z_stats "
            "norm_chain var_ready std_ready x1_ready x1_kept x1_ps x1t_ready scaled "
            "mix_r mix_k fk_ps r_ps relu_done sq_done gate_ready fv_ps gated_done z2_ready "
            "z2_stats shift_ready out_ready out_ready_act out_scaled out_ready_pool stored").split()}
        xt_ld = [sem(f"xt_ld{s}") for s in range(2)]
        rot_done = [sem(f"rot_done_{u}") for u in "qk"]
        hi_done = [sem(f"hi_done_{u}") for u in "qk"]
        rest_done = [sem(f"rest_done_{u}") for u in "qk"]
        mid_done = [sem(f"mid_done_{u}") for u in "qk"]
        lo_done = [sem(f"lo_done_{u}") for u in "qk"]
        parked = [[sem(f"parked_{u}{s}") for s in range(2)] for u in "qk"]
        qk_ld = [sem(f"qk_ld{c}") for c in range(NG)]
        max_ld = [sem(f"max_ld{c}") for c in range(NG)]

        block = ctx.enter_context(nc.Block())

        mul_of = [S["q_mul"], S["qs_mul"], S["k_mul"], S["ks_mul"]]
        ps_of = [S["q_ps"], S["qs_ps"], S["k_ps"], S["ks_ps"]]

        def turns(eng, turn, lead):
            first = 1 if lead < 3 else 0
            last = (B - lead) // 2 if lead >= 3 else B // 2 - 1
            for m in range(-lead, 2 * first):
                turn(m, m // 2, m % 2)
            with eng.Fori(first, last) as i:
                for s in range(2):
                    turn(2 * i + s, i, s)
            for m in range(2 * last, B):
                turn(m, m // 2, m % 2)

        def batch(m, i, s, lead):
            n = m + lead
            if isinstance(n, int) and not 0 <= n < B:
                return None
            return n, i + (s + lead) // 2, (s + lead) % 2

        def after(eng, semaphore, value):
            if not (isinstance(value, int) and value <= 0):
                eng.wait_ge(semaphore, value)

        def groups(eng, step):
            for b in (-1, 0):
                for c in range(NG):
                    step(b, c)
            with eng.Fori(1, B - 1) as b:
                for c in range(NG):
                    step(b, c)
            for c in range(NG):
                step(B - 1, c)

        def ahead(b, c, lead):
            bb, cc = b + (c + lead) // NG, (c + lead) % NG
            n = NG * bb + cc
            if isinstance(n, int) and not 0 <= n < NN:
                return None
            return n, bb, cc

        PARK = (32, 16)
        LOAD = 16 * 2 * PARTS

        BEFORE = [(2, 0, 4, 2), (3, 0, 2, 1), (3, 2, 2, 1), (1, 0, 4, 4)]

        @block.sync
        def _(sp):
            sp.dma_start(wq_t[:, :, :], w_q).then_inc(S["w_q_in"], 16)
            sp.dma_start(xt[:, 0, :], x_t[:, 0:T]).then_inc(xt_ld[0], 16)
            sp.dma_start(wk_t[:, :, :], w_k).then_inc(S["weights_in"], 16)
            sp.dma_start(cos[:, :], rope_cos).then_inc(S["rope_in"], 16)
            sp.dma_start(sin[:, :], rope_sin).then_inc(S["rope_in"], 16)
            sp.dma_start(wv_t[:, :], w_v).then_inc(S["weights_in"], 16)
            sp.dma_start(xt[:, 1, :], x_t[:, T:2 * T]).then_inc(xt_ld[1], 16)
            sp.dma_start(ident[:, :], eye).then_inc(S["consts_in"], 16)
            sp.dma_start(wo_t[:, :], w_out).then_inc(S["late_weights_in"], 16)
            sp.dma_start(ffn_t[:, :, :], w_ffn).then_inc(S["late_weights_in"], 16)
            sp.dma_start(mu[:, 0:1], mu_r.rearrange("(p a) -> p a", a=1)).then_inc(S["mu_in"], 16)
            sp.dma_start(mu[:, 1:2], mu_k.rearrange("(p a) -> p a", a=1)).then_inc(S["mu_in"], 16)
            sp.dma_start(z_all[:, :, :], x.rearrange("b (i p) d -> p (b i) d", p=128)).then_inc(S["z_in"], 16)

            def load(n, bb, cc):
                def rows(parts, lo):
                    return parts[bb, lo:lo + PARTS, 32 * cc:32 * cc + 32].rearrange("a (d g) t -> a d (g t)", g=G)
                for r in range(PARTS):
                    sp.dma_start(ka[24 * r:24 * r + 24, cc, :], rows(k_parts, 0)).then_inc(qk_ld[cc], 16)
                    sp.dma_start(qa[24 * r:24 * r + 24, cc, :], rows(q_parts, r)).then_inc(qk_ld[cc], 16)

            def park(m, i, s):
                done, far = batch(m, i, s, 0), batch(m, i, s, 2)
                if done and far:
                    n, ii, ss = far
                    sp.wait_ge(S["v_ps"], n - 1)
                    sp.dma_start(xt[:, ss, :], x_t[:, bass.ds(n * T, T)]).then_inc(xt_ld[ss], 16)
                if isinstance(m, int) and m >= B - 2:
                    if m == B - 2:
                        sp.wait_ge(S["ka_ones"], 1)
                        for u in range(2):
                            sp.wait_ge(parked[u][0], PARK[u])
                    for cc in range(2):
                        load(2 * (m - B + 2) + cc, 0, 2 * (m - B + 2) + cc)
                if done:
                    n, ii, ss = done
                    sp.wait_ge(lo_done[0], n + 1)
                    sp.dma_start(q_parts[n, 0:PARTS].rearrange("a p t -> p a t"),
                                 split[:, 0, ss]).then_inc(parked[0][ss], 16)
                    sp.dma_start(q_parts[n, PARTS:].rearrange("a p t -> p a t"),
                                 split[:, 0, ss, 0:PARTS - 1]).then_inc(parked[0][ss], 16)
                    sp.wait_ge(lo_done[1], n + 1)
                    sp.dma_start(k_parts[n].rearrange("a p t -> p a t"), split[:, 1, ss]).then_inc(parked[1][ss], 16)

            turns(sp, park, 1)
            def feed(b, c):
                g = ahead(b, c, 4)
                if g and not (isinstance(b, int) and b < 0):
                    if isinstance(b, int) and g[0] == NG:
                        for u in range(2):
                            for s in range(2):
                                sp.wait_ge(parked[u][s], PARK[u] * (B // 2))
                    sp.wait_ge(S["p2_ready"], 10 * (g[0] - 3))
                    load(*g)

            groups(sp, feed)

            with sp.Fori(0, B // 2) as i:
                sp.wait_ge(S["out_ready"], i + 1)
                sp.wait_ge(S["out_ready_act"], i + 1)
                sp.wait_ge(S["out_ready_pool"], i + 1)
                sp.dma_start(out_rows[i], z_all[:, bass.ds(2 * i * NB, 2 * NB), :]).then_inc(S["stored"], 16)
            sp.wait_ge(S["stored"], 16 * (B // 2))

        @block.tensor
        def _(pe):
            pe.wait_ge(S["w_q_in"], 16)

            def project(m, i, s):
                new = batch(m, i, s, 1)
                if not new:
                    return
                n, ii, ss = new
                pe.wait_ge(xt_ld[ss], 16 * (ii + 1))
                for a, w in enumerate((wq_t[:, 0, :], wq_t[:, 1, :], wk_t[:, 0, :], wk_t[:, 1, :])):
                    if isinstance(n, int) and n == 0 and a == 2:
                        pe.wait_ge(S["weights_in"], 32)
                    after(pe, mul_of[a], n)
                    pe.matmul(ps_qk[a], w, xt[:, ss, :], start=True, stop=True).then_inc(ps_of[a], 1)
                after(pe, S["v_ready"], n - 1)
                for j in range(NB):
                    mm = pe.matmul(ps_v[ss][:, 128 * j:128 * j + 128], xt[:, ss, 128 * j:128 * j + 128],
                                   wv_t[:, :], start=True, stop=True)
                mm.then_inc(S["v_ps"], 1)

            turns(pe, project, 1)

            for m in mul_of:
                pe.wait_ge(m, B)

            def diagonal_tile(g, t):
                n, bb, cc = g
                if t == 0:
                    after(pe, S["p1_reduced"], 4 * n)
                else:
                    pe.wait_ge(S["diag_copied"], 2 * n + 1)
                for i in range(2):
                    for h in range(G):
                        tok = T * h + 128 * (2 * t + i)
                        mm = pe.matmul(wide[1][:, 512 * i + 128 * h:512 * i + 128 * h + 128],
                                       qa[0:KR, cc, tok:tok + 128], ka[0:KR, cc, tok:tok + 128], start=True, stop=True)
                mm.then_inc(S["diag_ps"], 1)

            def before_tile(g, t):
                n, bb, cc = g
                if t == 0:
                    pe.wait_ge(qk_ld[cc], LOAD * (bb + 1))
                    after(pe, S["p1_reduced"], 4 * n - 1)
                elif t == 3:
                    pe.wait_ge(S["diag_copied"], 2 * n + 2)
                else:
                    pe.wait_ge(S["p1_reduced"], 4 * n + t)
                i, g0, heads, per = BEFORE[t]
                keys = 128 * i
                for h in range(heads):
                    at = 512 * (h // per) + keys * (h % per)
                    tok = T * (g0 + h)
                    mm = pe.matmul(wide[t // 3][:, at:at + keys], qa[0:KR, cc, tok + keys:tok + keys + 128],
                                   ka[0:KR, cc, tok:tok + keys], start=True, stop=True)
                mm.then_inc(S["p1_ready"], 1)

            def p2_tile(g, t):
                n, bb, cc = g
                if t == 0:
                    pe.wait_ge(max_ld[cc], 16 * (bb + 1))
                if not (isinstance(n, int) and n == 0 and t < 2):
                    pe.wait_ge(S["exp_done"], 10 * n + t - 1)

                def block_of(h, j, at):
                    tok = T * h
                    return pe.matmul(bank[t % 2][:, at:at + T - 128 * j],
                                     ka[0:KM, cc, tok + 128 * j:tok + 128 * j + 128],
                                     qa[0:KM, cc, tok + 128 * j:tok + T], start=True, stop=True)
                if t < 4:
                    mm = block_of(t, 0, 0)
                elif t < 8:
                    block_of(t - 4, 1, 0)
                    mm = block_of(t - 4, 3, 384)
                else:
                    block_of(2 * (t - 8), 2, 0)
                    mm = block_of(2 * (t - 8) + 1, 2, 256)
                mm.then_inc(S["p2_ready"], 1)

            def p_block(par, h, j):
                if j == 0:
                    return probs[:, par, h, :]
                if j == 1:
                    return probs[:, par, 4 + h, 0:384]
                if j == 3:
                    return probs[:, par, 4 + h, 384:512]
                return probs[:, par, 8 + h // 2, 256 * (h % 2):256 * (h % 2) + 256]

            def av(g, j):
                n, bb, cc = g
                pe.wait_ge(S["mask_done"], 3 * n + (1, 1, 3, 2)[j])
                if j == 0:
                    pe.wait_ge(S["v_slot"], n + 1)
                    pe.wait_ge(S["o_ready"], n)
                for h in range(G):
                    mm = pe.matmul(ps_o[32 * h:32 * h + 32, 128 * j:T], vs[:, cc, j, h, :],
                                   p_block(cc % 2, h, j), start=(j == 0), stop=(j == 2))
                if j == 2:
                    mm.then_inc(S["av_done"], 1)

            def max_transpose(g):
                n, bb, cc = g
                if isinstance(n, int) and n == 0:
                    pe.wait_ge(S["v_ready"], B)
                    pe.wait_ge(S["ident_cast"], 1)
                    pe.wait_ge(S["late_weights_in"], 32)
                pe.wait_ge(S["ns_ready"], n + 1)
                pe.transpose(ps_m[:, 0:64].bitcast(bf16), nsplit[:, cc % 2, :], ident_b[:, :]).then_inc(S["mt_ps"], 1)

            def o_transposes(g):
                n, bb, cc = g
                pe.wait_ge(S["o_ready"], n + 1)
                for j in range(NB):
                    mm = pe.transpose(ps_m[:, 128 * j:128 * j + 128], o_raw[:, 128 * j:128 * j + 128], ident[:, :])
                mm.then_inc(S["ot_raw_ps"], 1)

            def step(b, c):
                new, scored, mult, maxed, post = (ahead(b, c, k) for k in (4, 2, 1, 3, 0))

                def p1(t):
                    if new:
                        before_tile(new, t)

                def diagonal(t):
                    if new:
                        diagonal_tile(new, t)

                def p2(t):
                    if scored:
                        p2_tile(scored, t)

                def pv(j):
                    if mult:
                        av(mult, j)

                def max_part():
                    if maxed:
                        if post:
                            after(pe, S["o_normed"], post[0])
                            if c == 0:
                                after(pe, S["z_ready"], post[1])
                        max_transpose(maxed)

                def post_part():
                    if post:
                        if maxed:
                            pe.wait_ge(S["mt_ready"], maxed[0] + 1)
                        else:
                            pe.wait_ge(S["o_normed"], post[0])
                        o_transposes(post)

                def batch_transposes():
                    pe.wait_ge(S["o_normed"], post[0] + 1)
                    for j in range(NB):
                        mm = pe.transpose(ps_m[:, 128 * j:128 * j + 128],
                                          o_tok[:, j].rearrange("p h d -> p (h d)"), ident[:, :])
                    mm.then_inc(S["otok_ps"], 1)

                def batch_projection():
                    pe.wait_ge(S["ot_ready"], post[1] + 1)
                    for j in range(NB):
                        mm = pe.matmul(ps_m[:, 128 * j:128 * j + 128], o_t[:, 128 * j:128 * j + 128],
                                       wo_t[:, :], start=True, stop=True)
                    mm.then_inc(S["y_ps"], 1)

                whole = post and c == NG - 1
                p2(0)
                p1(0)
                p2(1)
                diagonal(0)
                pv(0)
                p2(2)
                p2(3)
                p1(1)
                pv(1)
                max_part()
                p2(4)
                diagonal(1)
                pv(3)
                p2(5)
                p1(2)
                post_part()
                p2(6)
                p2(7)
                p1(3)
                if whole:
                    batch_transposes()
                p2(8)
                pv(2)
                p2(9)
                if whole:
                    batch_projection()

            groups(pe, step)

            pe.wait_ge(S["exp_done"], 10 * NN)

            def channel_mix(m, i, s):
                new, mid, old = (batch(m, i, s, k) for k in (2, 1, 0))
                if isinstance(m, int) and m == -1:
                    pe.wait_ge(S["z_ready"], B)
                if mid:
                    n, _, ss = mid
                    pe.wait_ge(S["mix_k"], n + 1)
                    after(pe, S["relu_done"], n - 1)
                    pe.matmul(ps_k[ss], ffn_t[:, 1, :], mixed[:, ss, 1, :], start=True, stop=True).then_inc(S["fk_ps"], 1)
                if new:
                    n, _, ss = new
                    pe.wait_ge(S["x1_ready"], n + 1)
                    after(pe, S["x1t_ready"], n - 1)
                    for j in range(NB):
                        mm = pe.transpose(ps_x1t[ss][:, 128 * j:128 * j + 128], x1[:, ss, j, :], ident[:, :])
                    mm.then_inc(S["x1_ps"], 1)
                if old:
                    n, _, ss = old
                    pe.wait_ge(S["sq_done"], n + 1)
                    after(pe, S["gated_done"], n - 1)
                    for j in range(NB):
                        mm = pe.matmul(ps_fv[ss][:, 128 * j:128 * j + 128], k_sq[:, ss, 128 * j:128 * j + 128],
                                       ffn_t[:, 2, :], start=True, stop=True)
                    mm.then_inc(S["fv_ps"], 1)
                if mid:
                    n, _, ss = mid
                    pe.wait_ge(S["mix_r"], n + 1)
                    after(pe, S["gate_ready"], n - 1)
                    for j in range(NB):
                        mm = pe.matmul(ps_r[ss][:, 128 * j:128 * j + 128], mixed[:, ss, 0, 128 * j:128 * j + 128],
                                       ffn_t[:, 0, :], start=True, stop=True)
                    mm.then_inc(S["r_ps"], 1)

            turns(pe, channel_mix, 2)

        @block.scalar
        def _(act):
            def copy(dst, src):
                return act.activation(dst, src, ACT.Copy)

            def root(k, lo, hi):
                act.wait_ge(S["var_ready"], k)
                act.activation(std[:, lo * NB:hi * NB], var[:, lo * NB:hi * NB], ACT.Sqrt).then_inc(S["std_ready"], 1)

            def split_parts(m, i, s):
                n, ii, ss = batch(m, i, s, 0)

                def first(u):
                    act.wait_ge(rot_done[u], n + 1)
                    after(act, parked[u][ss], PARK[u] * ii)
                    copy(split[:, u, ss, 0], rot[:, ss, u, :]).then_inc(hi_done[u], 1)

                def second(u):
                    act.wait_ge(rest_done[u], n + 1)
                    copy(split[:, u, ss, 1], rest[:, u, :]).then_inc(mid_done[u], 1)

                first(0)
                second(0)
                first(1)
                act.wait_ge(S["v_ps"], n + 1)
                copy(v_all[:, bass.ds(n * NB, NB), :].rearrange("p i d -> p (i d)"), ps_v[ss][:, :]).then_inc(S["v_ready"], 1)
                second(1)

            turns(act, split_parts, 0)

            def step(b, c):
                new, maxed, scored, mult, post = (ahead(b, c, k) for k in (4, 3, 2, 1, 0))

                def exps(t0, t1):
                    if not scored:
                        return
                    n, bb, cc = scored
                    for t in range(t0, t1):
                        if t == 0 and not (isinstance(n, int) and n < 2):
                            act.wait_ge(S["av_done"], n - 1)
                        act.wait_ge(S["p2_ready"], 10 * n + t + 1)
                        act.activation(probs[:, cc % 2, t, :], bank[t % 2][:, :], ACT.Exp,
                                       scale=SCALE).then_inc(S["exp_done"], 1)

                if isinstance(b, int) and b == B - 1 and c == 2:
                    root(1, 0, B - 1)

                def diagonal_out(h):
                    if new:
                        n = new[0]
                        act.wait_ge(S["diag_ps"], 2 * n + h + 1)
                        after(act, S["diag_reduced"], 2 * n + h - 1)
                        copy(diag[:, h].rearrange("p x k -> p (x k)"), wide[1][:, :]).then_inc(S["diag_copied"], 1)

                exps(0, 2)
                diagonal_out(0)
                exps(2, 5)
                diagonal_out(1)
                exps(5, 6)
                if maxed:
                    n, bb, cc = maxed
                    act.wait_ge(S["mt_ready"], n + 1)
                    act.dma_start(qa[KR:KM, cc, :].rearrange("a (x q) -> a x q", q=128),
                                  nmax_t[:, cc % 2, :]).then_inc(max_ld[cc], 16)
                exps(6, 8)
                if post and c == NG - 1:
                    act.wait_ge(S["otok_ps"], post[1] + 1)
                    act.wait_ge(S["y_ps"], post[1])
                    copy(o_t[:, :], ps_m[:, :]).then_inc(S["ot_ready"], 1)
                exps(8, 10)
                if mult:
                    n = mult[0]
                    act.wait_ge(S["av_done"], n + 1)
                    act.wait_ge(S["ot_raw_ps"], n)
                    copy(o_raw[:, :], ps_o[:, :]).then_inc(S["o_ready"], 1)

            groups(act, step)

            act.wait_ge(S["mu_in"], 32)

            def mix(m, i, s):
                new, mid = (batch(m, i, s, k) for k in (2, 1))
                if isinstance(m, int) and m == -1:
                    root(2, B - 1, B)
                if mid:
                    n, _, ss = mid
                    act.wait_ge(S["fk_ps"], n + 1)
                    after(act, S["sq_done"], n - 1)
                    act.activation(k_relu[:, ss, :], ps_k[ss], ACT.Relu).then_inc(S["relu_done"], 1)
                if new:
                    n, _, ss = new
                    act.wait_ge(S["x1_ps"], n + 1)
                    after(act, S["mix_r"], n - 1)
                    copy(x1_t[:, ss, 1:T + 1], ps_x1t[ss][:, :]).then_inc(S["x1t_ready"], 1)
                    act.wait_ge(S["x1t_ready"], n + 1)
                    for a, name in ((1, "mix_k"), (0, "mix_r")):
                        after(act, S[name], n)
                        act.activation(scaled[:, a, :], x1_t[:, ss, 1:T + 1], ACT.Copy,
                                       scale=mu[:, a:a + 1]).then_inc(S["scaled"], 1)
                if mid:
                    n, _, ss = mid
                    act.wait_ge(S["r_ps"], n + 1)
                    after(act, S["gated_done"], n - 1)
                    act.activation(gate[:, ss, :], ps_r[ss], ACT.Sigmoid).then_inc(S["gate_ready"], 1)

            turns(act, mix, 2)
            root(3, 0, B - 2)
            act.wait_ge(S["shift_ready"], 1)

            def finish(i):
                for j in range(3, 6):
                    at = 2 * i * NB + j
                    z = z_all[:, bass.ds(at, 1), :].rearrange("p a d -> p (a d)")
                    last = act.activation(z, z, ACT.Identity, scale=rstd[:, bass.ds(at, 1)],
                                          bias=shift[:, bass.ds(at, 1)])
                last.then_inc(S["out_ready_act"], 1)

            with act.Fori(0, B // 2 - 1) as i:
                finish(i)
            root(4, B - 2, B)
            act.wait_ge(S["shift_ready"], 2)
            finish(B // 2 - 1)

        @block.vector
        def _(dve):
            dve.memset(vs[:, :, :, :, :], 1.0).then_inc(S["fills"], 1)
            dve.memset(x1_t[:, :, 0:1], 0.0).then_inc(S["fills"], 1)
            dve.memset(nsplit[:, :, :], 0.0).then_inc(S["fills"], 1)
            dve.wait_ge(S["rope_in"], 32)

            def rotate(m, i, s):
                new, old = batch(m, i, s, 1), batch(m, i, s, 0)
                for u in range(2):
                    if old:
                        n, _, ss = old
                        dve.wait_ge(hi_done[u], n + 1)
                        after(dve, lo_done[u], n)
                        dve.tensor_tensor(rest[:, u, :], rot[:, ss, u, :], split[:, u, ss, 0], ALU.subtract).then_inc(rest_done[u], 1)
                    if new:
                        n = new[0]
                        for a in (2 * u, 2 * u + 1):
                            dve.wait_ge(ps_of[a], n + 1)
                            after(dve, rot_done[u], n)
                            dst, table = ((rot_a, cos), (rot_b, sin))[a % 2]
                            dve.tensor_tensor(dst[:, u, :], ps_qk[a], table[:, :], ALU.mult).then_inc(mul_of[a], 1)

            turns(dve, rotate, 1)
            dve.wait_ge(S["consts_in"], 16)
            dve.tensor_copy(ident_b[:, :], ident[:, :]).then_inc(S["ident_cast"], 1)
            dve.wait_ge(S["mu_in"], 32)
            dve.tensor_scalar(mu_rest[:, :], mu[:, :], -1.0, 1.0, ALU.mult, ALU.add).then_inc(S["mu_ready"], 1)

            def step(b, c):
                new, maxed, post = (ahead(b, c, k) for k in (4, 3, 0))

                def statistics(bb):
                    dve.wait_ge(S["z_ready"], bb + 1)
                    for j in range(NB):
                        dve.bn_stats(stats[:, bass.ds(bb * NB + j, 1), :].rearrange("p a k -> p (a k)"),
                                     z_all[:, bass.ds(bb * NB + j, 1), :].rearrange("p a d -> p (a d)")).then_inc(S["z_stats"], 1)

                def reduce(t):
                    n, bb, cc = new
                    if t == 0:
                        after(dve, S["nmax_ready"], n)
                    dve.wait_ge(S["p1_ready"], 4 * n + t + 1)
                    i, g0, heads, per = BEFORE[t]
                    keys = 128 * i
                    src = wide[t // 3][:, :].rearrange("p (k n) -> p k n", n=512)[:, :, 0:keys]
                    if per > 1:
                        src = wide[t // 3][:, 0:keys * heads].rearrange("p (h m) -> p h m", m=keys)
                    dve.tensor_reduce(nbefore[:, g0:g0 + heads, i - 1], src, AX.X, ALU.max,
                                      negate=True).then_inc(S["p1_reduced"], 1)

                def reduce_diagonal(h):
                    n, bb, cc = new
                    if h == 0 and not (isinstance(n, int) and n < 2):
                        dve.wait_ge(S["ns_ready"], n - 1)
                    dve.wait_ge(S["diag_masked"], 2 * n + h + 1)
                    dst = nmax[:, cc % 2, :].rearrange("p (g i) -> p i g", i=NB)[:, 2 * h:2 * h + 2, :]
                    dve.tensor_reduce(dst, diag[:, h].rearrange("p (i g) k -> p i g k", i=2), AX.X, ALU.max,
                                      negate=True).then_inc(S["diag_reduced"], 1)

                def combine():
                    n, bb, cc = new
                    dve.wait_ge(S["p1_reduced"], 4 * n + 4)
                    dve.wait_ge(S["diag_reduced"], 2 * n + 2)
                    both = nmax[:, cc % 2, :].rearrange("p (g i) -> p g i", i=NB)[:, :, 1:]
                    dve.tensor_tensor(both, both, nbefore[:, :, :], ALU.min).then_inc(S["nmax_ready"], 1)

                if new:
                    reduce(0)
                if c == 0 and not (isinstance(b, int) and b < 1):
                    statistics(b - 1)
                if new:
                    reduce(1)
                if maxed:
                    n, bb, cc = maxed
                    dve.wait_ge(S["mt_ps"], n + 1)
                    if not (isinstance(n, int) and n < 2):
                        b2, c2 = bb + (cc - 2) // NG, (cc - 2) % NG
                        dve.wait_ge(max_ld[c2], 16 * (b2 + 1))
                    dve.tensor_copy(nmax_t[:, cc % 2, :], ps_m[0:PARTS * G * NB, 0:64].bitcast(bf16)).then_inc(S["mt_ready"], 1)
                if new:
                    reduce_diagonal(0)
                    reduce(2)
                if post:
                    n, bb, cc = post
                    o = ps_m[:, :].rearrange("p (j g w) -> p j g w", j=NB, g=G)
                    dve.wait_ge(S["ot_raw_ps"], n + 1)
                    dve.wait_ge(S["o_normed"], n)
                    dve.wait_ge(S["otok_ps"], bb)
                    dve.reciprocal(den_inv[:, :, :], o[:, :, :, HD]).then_inc(S["den_ready"], 1)
                    dve.wait_ge(S["den_ready"], n + 1)
                    dve.tensor_tensor(o_tok[:, :, G * cc:G * cc + G, :], o[:, :, :, 0:HD],
                                      den_inv[:, :, :].unsqueeze(3).to_broadcast((128, NB, G, HD)), ALU.mult).then_inc(S["o_normed"], 1)
                if new:
                    reduce(3)
                    reduce_diagonal(1)
                    combine()
                if isinstance(b, int) and b == B - 1:
                    if c == 1:
                        dve.wait_ge(S["z_stats"], (B - 1) * NB)
                        variances(0, B - 1)
                    if c == 2:
                        inverse_roots(1, 0, B - 1)
                    if c == 3:
                        mix(-3, -2, 1)
                if post and c == NG - 1:
                    bb = post[1]
                    if isinstance(bb, int) and bb == 0 or not isinstance(bb, int):
                        dve.wait_ge(S["z_in"], 16)
                    dve.wait_ge(S["y_ps"], bb + 1)
                    z = z_all[:, bass.ds(bb * NB, NB), :]
                    dve.tensor_tensor(z, ps_m[:, :].rearrange("p (i d) -> p i d", i=NB), z, ALU.add).then_inc(S["z_ready"], 1)
                    if isinstance(bb, int) and bb == B - 1:
                        statistics(bb)

            chain = [0]

            def link(ins):
                chain[0] += 1
                ins.then_inc(S["norm_chain"], 1)
                dve.wait_ge(S["norm_chain"], chain[0])

            def variances(lo, hi):
                at = slice(lo * NB, hi * NB)
                m_even, q_even, m_odd, q_odd = (stats[:, at, a] for a in (1, 2, 4, 5))
                h, v = half[:, at], var[:, at]
                link(dve.tensor_tensor(h, m_even, m_odd, ALU.subtract))
                link(dve.tensor_scalar(h, h, 0.5, None, ALU.mult))
                link(dve.tensor_tensor(mean[:, at], h, m_odd, ALU.add))
                link(dve.tensor_tensor(h, h, h, ALU.mult))
                link(dve.tensor_tensor(v, q_even, q_odd, ALU.add))
                link(dve.tensor_scalar(v, v, 1.0 / D, EPS, ALU.mult, ALU.add))
                dve.tensor_tensor(v, v, h, ALU.add).then_inc(S["var_ready"], 1)

            def inverse_roots(k, lo, hi):
                dve.wait_ge(S["std_ready"], k)
                link(dve.reciprocal(rstd[:, lo * NB:hi * NB], std[:, lo * NB:hi * NB]))

            def shifts(lo, hi):
                at = slice(lo * NB, hi * NB)
                link(dve.tensor_tensor(half[:, at], mean[:, at], rstd[:, at], ALU.mult))
                dve.tensor_scalar(shift[:, at], half[:, at], -1.0, None, ALU.mult).then_inc(S["shift_ready"], 1)

            def normalise(n, j, dst):
                at = n * NB + j
                return dve.tensor_scalar(dst, z_all[:, bass.ds(at, 1), :].rearrange("p a d -> p (a d)"),
                                         mean[:, bass.ds(at, 1)], rstd[:, bass.ds(at, 1)], ALU.subtract, ALU.mult)

            def mix(m, i, s):
                new, mid, old, summed = (batch(m, i, s, k) for k in (3, 2, 1, 0))

                def mixed_input(a, name, nth):
                    n, _, ss = mid
                    after(dve, S["r_ps"], n - 1)
                    dve.wait_ge(S["scaled"], 2 * n + nth)
                    dve.scalar_tensor_tensor(out=mixed[:, ss, a, :], in0=x1_t[:, ss, 0:T],
                                             scalar=mu_rest[:, a:a + 1], in1=scaled[:, a, :],
                                             op0=ALU.mult, op1=ALU.add).then_inc(S[name], 1)

                if isinstance(m, int) and m == -2:
                    dve.wait_ge(S["z_stats"], B * NB)
                    variances(B - 1, B)
                if isinstance(m, int) and m == -1:
                    inverse_roots(2, B - 1, B)
                if isinstance(m, int) and m == B - 2:
                    dve.wait_ge(S["z2_stats"], (B - 2) * NB)
                    variances(0, B - 2)
                if mid:
                    mixed_input(1, "mix_k", 1)
                if new:
                    n, _, ss = new
                    after(dve, S["x1_kept"], n - 1)
                    after(dve, S["x1_ps"], n - 1)
                    for j in range(NB):
                        last = normalise(n, j, x1[:, ss, j, :])
                    last.then_inc(S["x1_ready"], 1)
                if mid:
                    mixed_input(0, "mix_r", 2)
                if summed:
                    n, _, ss = summed
                    dve.wait_ge(S["z2_ready"], n + 1)
                    for j in range(NB):
                        dve.bn_stats(stats[:, bass.ds(n * NB + j, 1), :].rearrange("p a k -> p (a k)"),
                                     z_all[:, bass.ds(n * NB + j, 1), :].rearrange("p a d -> p (a d)")).then_inc(S["z2_stats"], 1)
                if old:
                    n, _, ss = old
                    dve.wait_ge(S["fv_ps"], n + 1)
                    dve.wait_ge(S["gate_ready"], n + 1)
                    after(dve, S["z2_ready"], n)
                    dve.tensor_tensor(gated[:, :], ps_fv[ss][:, :], gate[:, ss, :], ALU.mult).then_inc(S["gated_done"], 1)

            groups(dve, step)

            dve.wait_ge(S["mu_ready"], 1)

            def mix_rest(m, i, s):
                if not (isinstance(m, int) and m == -3):
                    mix(m, i, s)

            turns(dve, mix_rest, 3)
            dve.wait_ge(S["z2_stats"], B * NB)
            variances(B - 2, B)
            inverse_roots(3, 0, B - 2)
            shifts(0, B - 2)

            def finish(i):
                for j in range(3):
                    last = normalise(2 * i, j, z_all[:, bass.ds(2 * i * NB + j, 1), :].rearrange("p a d -> p (a d)"))
                last.then_inc(S["out_ready"], 1)

            with dve.Fori(0, B // 2 - 1) as i:
                finish(i)
            inverse_roots(4, B - 2, B)
            shifts(B - 2, B)
            finish(B // 2 - 1)

        @block.gpsimd
        def _(pool):
            def wait(semaphore, value):
                pool.wait_ge(semaphore, value)
                pool.nop(nofuse=True)

            pool.memset(ka[64:KM, :, :].bitcast(f32), TWO_ONES).then_inc(S["ka_ones"], 1)
            pool.wait_ge(S["ka_ones"], 1)

            def rotate(m, i, s):
                new, old = batch(m, i, s, 1), batch(m, i, s, 0)
                for u in range(2):
                    if old:
                        n, _, ss = old
                        pool.wait_ge(mid_done[u], n + 1)
                        pool.tensor_tensor(split[:, u, ss, 2], rest[:, u, :], split[:, u, ss, 1], ALU.subtract).then_inc(lo_done[u], 1)
                    if new:
                        n, _, ss = new
                        pool.wait_ge(mul_of[2 * u], n + 1)
                        pool.wait_ge(mul_of[2 * u + 1], n + 1)
                        after(pool, rest_done[u], n - 1)
                        pool.tensor_tensor(rot[:, ss, u, :], rot_a[:, u, :], rot_b[:, u, :], ALU.add).then_inc(rot_done[u], 1)

            turns(pool, rotate, 1)
            pool.wait_ge(S["v_ready"], B)
            pool.wait_ge(S["fills"], 3)

            def step(b, c):
                new, maxed, scored = (ahead(b, c, k) for k in (4, 3, 2))
                if new:
                    n, bb, cc = new
                    if not (isinstance(n, int) and n < 4):
                        wait(S["av_done"], n - 3)
                    src = v_all[:, bass.ds(bb * NB, NB), 32 * cc:32 * cc + 32].rearrange("p j (g d) -> p j g d", g=G)
                    pool.tensor_copy(vs[:, cc, :, :, 0:HD], src).then_inc(S["v_slot"], 1)
                if maxed:
                    n, bb, cc = maxed
                    nm, rest_, parts = nmax[:, cc % 2, :], nmax_rest[:, :], nsplit[:, cc % 2, :]
                    wait(S["nmax_ready"], n + 1)
                    if not (isinstance(n, int) and n < 2):
                        wait(S["mt_ps"], n - 1)
                    pool.tensor_copy(parts[:, 0:16], nm).then_inc(S["ns_chain"], 1)
                    pool.wait_ge(S["ns_chain"], 3 * n + 1)
                    pool.tensor_tensor(rest_, nm, parts[:, 0:16], ALU.subtract).then_inc(S["ns_chain"], 1)
                    wait(S["ns_chain"], 3 * n + 2)
                    pool.tensor_copy(parts[:, 16:32], rest_).then_inc(S["ns_chain"], 1)
                    pool.wait_ge(S["ns_chain"], 3 * n + 3)
                    pool.tensor_tensor(parts[:, 32:48], rest_, parts[:, 16:32], ALU.subtract).then_inc(S["ns_ready"], 1)
                if new:
                    n, bb, cc = new
                    for h in range(2):
                        wait(S["diag_copied"], 2 * n + h + 1)
                        pool.affine_select(out=diag[:, h], in_=diag[:, h], compare_op=ALU.is_ge, fill=NEG, base=0,
                                           pattern=[[0, 2 * G], [-1, 128]],
                                           channel_multiplier=1).then_inc(S["diag_masked"], 1)
                if scored:
                    n, bb, cc = scored
                    def keep_causal(view):
                        pool.affine_select(out=view, in_=view, compare_op=ALU.is_ge, fill=0.0, base=0,
                                           pattern=[[0, view.shape[1]], [1, 128]],
                                           channel_multiplier=-1).then_inc(S["mask_done"], 1)
                    wait(S["exp_done"], 10 * n + 8)
                    keep_causal(probs[:, cc % 2, 0:8, 0:128])
                    keep_causal(probs[:, cc % 2, 4:8, 384:512])
                    wait(S["exp_done"], 10 * n + 10)
                    keep_causal(probs[:, cc % 2, 8:10, :].rearrange("p t (k q) -> p (t k) q", k=2)[:, :, 0:128])

            groups(pool, step)

            def mix(m, i, s):
                new, mid, old = (batch(m, i, s, k) for k in (2, 1, 0))
                if new:
                    n, _, ss = new
                    wait(S["x1_ready"], n + 1)
                    pool.tensor_copy(z_all[:, bass.ds(n * NB, NB), :].rearrange("p i d -> p (i d)"),
                                     x1[:, ss].rearrange("p i d -> p (i d)")).then_inc(S["x1_kept"], 1)
                if mid:
                    n, _, ss = mid
                    pool.wait_ge(S["relu_done"], n + 1)
                    after(pool, S["fv_ps"], n - 1)
                    pool.tensor_tensor(k_sq[:, ss, :], k_relu[:, ss, :], k_relu[:, ss, :], ALU.mult).then_inc(S["sq_done"], 1)
                if old:
                    n, _, ss = old
                    pool.wait_ge(S["x1_kept"], n + 1)
                    pool.wait_ge(S["gated_done"], n + 1)
                    z = z_all[:, bass.ds(n * NB, NB), :].rearrange("p i d -> p (i d)")
                    pool.tensor_tensor(z, gated[:, :], z, ALU.add).then_inc(S["z2_ready"], 1)

            turns(pool, mix, 2)

            def finish(i):
                at = 2 * i * NB + 6
                z = z_all[:, bass.ds(at, 2), :]

                def of_token(a):
                    return a[:, bass.ds(at, 2)].unsqueeze(2).to_broadcast((128, 2, 128))
                pool.tensor_tensor(z, z, of_token(rstd), ALU.mult).then_inc(S["out_scaled"], 1)
                pool.wait_ge(S["out_scaled"], i + 1)
                pool.tensor_tensor(z, z, of_token(shift), ALU.add).then_inc(S["out_ready_pool"], 1)

            pool.wait_ge(S["shift_ready"], 1)
            with pool.Fori(0, B // 2 - 1) as i:
                finish(i)
            pool.wait_ge(S["shift_ready"], 2)
            finish(B // 2 - 1)


def shape_constants():
    import numpy as np
    freqs = np.float32(1.0) / np.float32(10000.0) ** (np.arange(0, HD, 2, dtype=np.float32) / np.float32(HD))
    angles = np.outer(np.arange(T, dtype=np.float32), freqs.astype(np.float32)).astype(np.float32)
    d_of_row = np.arange(128) // G % HD
    cos = np.cos(angles).T[d_of_row // 2]
    sin = np.sin(angles).T[d_of_row // 2] * np.where(d_of_row % 2, 1.0, -1.0)[:, None]
    eye = np.eye(128)
    return {n: np.ascontiguousarray(a, dtype=np.float32)
            for n, a in (("rope_cos", cos), ("rope_sin", sin), ("eye", eye))}


def kernel(L0_attn_x, L0_attn_W_qkv, L0_attn_W_out, L0_ffn_W_r, L0_ffn_W_k, L0_ffn_W_v, L0_ffn_mu_r, L0_ffn_mu_k):
    import numpy as _np
    import concourse.bacc as _bacc
    from concourse import mybir as _mybir
    from concourse.bass_utils import run_bass_kernel_spmd as _run

    nc = _bacc.Bacc("TRN2", target_bir_lowering=False, num_devices=1)
    arrays, args = {}, []
    wq, wk, wv = (_np.asarray(L0_attn_W_qkv)[D * a:D * a + D] for a in range(3))
    order = _np.arange(D).reshape(NG, G, HD).transpose(0, 2, 1)
    swapped = order.reshape(NG, HD // 2, 2, G)[:, :, ::-1]
    rows = _np.stack([order.reshape(-1), swapped.reshape(-1)])
    given = [("x", L0_attn_x), ("x_t", _np.asarray(L0_attn_x).reshape(B * T, D).T),
             ("w_q", wq[rows].transpose(2, 0, 1)), ("w_k", wk[rows].transpose(2, 0, 1)), ("w_v", wv.T),
             ("w_out", _np.asarray(L0_attn_W_out).T),
             ("w_ffn", _np.stack([_np.asarray(L0_ffn_W_r).T, _np.asarray(L0_ffn_W_k).T,
                                  _np.asarray(L0_ffn_W_v).T], axis=1)),
             ("mu_r", L0_ffn_mu_r), ("mu_k", L0_ffn_mu_k)]
    for name, a in given + list(shape_constants().items()):
        a = _np.ascontiguousarray(a)
        arrays[f"in_{name}"] = a
        args.append(nc.dram_tensor(f"in_{name}", a.shape, _mybir.dt.from_np(a.dtype), kind="ExternalInput").ap())
    for name, parts in (("q_parts", 2 * PARTS - 1), ("k_parts", PARTS)):
        args.append(nc.dram_tensor(name, (B, parts, 128, T), _mybir.dt.bfloat16, kind="Internal").ap())
    args.append(nc.dram_tensor("out_0", (B, T, D), _mybir.dt.float32, kind="ExternalOutput").ap())
    attention_block(nc, *args)
    r = _run(nc, [arrays], core_ids=[0])
    return r.results[0]["out_0"]
```
